# Optimizing a Trainium2 kernel written in Bass

```python
import numpy as np
import jax
import jax.numpy as jnp

def _softmax(x, axis=-1):
    return jax.nn.softmax(x, axis=axis)

def _gelu(x):
    return jax.nn.gelu(x, approximate=True)

def _silu(x):
    return jax.nn.silu(x)

def _sigmoid(x):
    return jax.nn.sigmoid(x)

def _layernorm(x, axis=-1, eps=1e-05):
    m = jnp.mean(x, axis=axis, keepdims=True)
    v = jnp.var(x, axis=axis, keepdims=True)
    return (x - m) / jnp.sqrt(v + eps)

def _scatter_add(tgt, idx, src, axis=0):
    return tgt.at[idx].add(src)

def _segment_sum(src, seg, n):
    return jax.ops.segment_sum(src, seg, n)
kernel_name = 'mk_xattn_seq_d1_seqx_r8_9db978'

def setup_inputs(seed: int=0):
    np.random.seed(seed)
    _w = jnp.asarray

    def _rec_inputs():
        import jax
        import jax.numpy as jnp
        _rk = jax.random.key(seed)
        x = -0.0005207 + 1.001 * jax.random.normal(jax.random.fold_in(_rk, 1), (8, 56, 256), jnp.float32)
        _lenS = 56 - jax.random.randint(jax.random.fold_in(_rk, 7), (8,), 0, max(1, 56 // 4) + 1, jnp.int32)
        _lenS2 = 1500 - jax.random.randint(jax.random.fold_in(_rk, 8), (8,), 0, max(1, 1500 // 4) + 1, jnp.int32)
        _ctx_2048P = jax.random.normal(jax.random.fold_in(_rk, 11), (8, 16, 256), jnp.float32)
        _ctx_2048c = jax.random.dirichlet(jax.random.fold_in(_rk, 511), 0.3 * jnp.ones((16,), jnp.float32), (8, 1500))
        _ctx_2048t = jnp.einsum('bsk,bkd->bsd', _ctx_2048c, _ctx_2048P)
        _ctx_2048t = _ctx_2048t * jax.lax.rsqrt(jnp.mean(jnp.square(_ctx_2048t)) + 1e-12) * 0.953939
        ctx_2048 = 2.81802e-05 + 1.00001 * (_ctx_2048t + 0.3 * jax.random.normal(jax.random.fold_in(_rk, 611), (8, 1500, 256), jnp.float32))
        return (x, ctx_2048)
    x, ctx_2048 = _rec_inputs()

    def _L0_xattn_setup():
        import jax, jax.numpy as jnp
        import numpy as np
        B, Q, S1, S2 = (4, 32, 256, 256)
        D, H, K, F = (256, 16, 128, 1024)
        LN_EPS = 1e-05

        def _layer_norm(x, scale, offset):
            mu = jnp.mean(x, axis=-1, keepdims=True)
            var = jnp.var(x, axis=-1, keepdims=True)
            return (x - mu) * jax.lax.rsqrt(var + LN_EPS) * scale + offset

        def _cross_attention(q_in, kv_in, wq, bq, wk, bk, wv, bv, wo, bo, bias_k, bias_v):
            b, q_len, _ = q_in.shape
            t = kv_in.shape[1]
            qh = (q_in @ wq + bq).reshape(b, q_len, H, K)
            kh = (kv_in @ wk + bk).reshape(b, t, H, K)
            vh = (kv_in @ wv + bv).reshape(b, t, H, K)
            kh = jnp.concatenate([kh, jnp.broadcast_to(bias_k, (b, 1, H, K))], axis=1)
            vh = jnp.concatenate([vh, jnp.broadcast_to(bias_v, (b, 1, H, K))], axis=1)
            scale = jnp.sqrt(jnp.asarray(K, q_in.dtype))
            logits = jnp.einsum('bqhk,bthk->bhqt', qh, kh) / scale
            weights = jax.nn.softmax(logits, axis=-1)
            ctx = jnp.einsum('bhqt,bthk->bqhk', weights, vh).reshape(b, q_len, H * K)
            return ctx @ wo + bo

        def _forward(x, xf_1, xf_2, ln1_scale, ln1_offset, wq1, bq1, wk1, bk1, wv1, bv1, wo1, bo1, bias_k1, bias_v1, ln2_scale, ln2_offset, wq2, bq2, wk2, bk2, wv2, bv2, wo2, bo2, bias_k2, bias_v2, ln_mlp_scale, ln_mlp_offset, w_fc1, b_fc1, w_fc2, b_fc2):
            res = x
            h = _layer_norm(x, ln1_scale, ln1_offset)
            x = res + _cross_attention(h, xf_1, wq1, bq1, wk1, bk1, wv1, bv1, wo1, bo1, bias_k1, bias_v1)
            res = x
            h = _layer_norm(x, ln2_scale, ln2_offset)
            x = res + _cross_attention(h, xf_2, wq2, bq2, wk2, bk2, wv2, bv2, wo2, bo2, bias_k2, bias_v2)
            h = _layer_norm(x, ln_mlp_scale, ln_mlp_offset)
            h = jax.nn.gelu(h @ w_fc1 + b_fc1, approximate=False) @ w_fc2 + b_fc2
            return x + h
        key = jax.random.key(seed)
        ks = iter(jax.random.split(key, 64))

        def rn(shape, s=0.02):
            return jax.random.normal(next(ks), shape, jnp.float32) * s
        inp = {'x': rn((B, Q, D), 1.0), 'xf_1': rn((B, S1, D), 1.0), 'xf_2': rn((B, S2, D), 1.0)}
        for i in (1, 2):
            inp[f'ln{i}_scale'] = jnp.ones((D,), jnp.float32)
            inp[f'ln{i}_offset'] = jnp.zeros((D,), jnp.float32)
            inp[f'wq{i}'] = rn((D, H * K))
            inp[f'bq{i}'] = jnp.zeros((H * K,), jnp.float32)
            inp[f'wk{i}'] = rn((D, H * K))
            inp[f'bk{i}'] = jnp.zeros((H * K,), jnp.float32)
            inp[f'wv{i}'] = rn((D, H * K))
            inp[f'bv{i}'] = jnp.zeros((H * K,), jnp.float32)
            inp[f'wo{i}'] = rn((H * K, D))
            inp[f'bo{i}'] = jnp.zeros((D,), jnp.float32)
            inp[f'bias_k{i}'] = rn((1, 1, H, K))
            inp[f'bias_v{i}'] = rn((1, 1, H, K))
        inp['ln_mlp_scale'] = jnp.ones((D,), jnp.float32)
        inp['ln_mlp_offset'] = jnp.zeros((D,), jnp.float32)
        inp['w_fc1'] = rn((D, F))
        inp['b_fc1'] = jnp.zeros((F,), jnp.float32)
        inp['w_fc2'] = rn((F, D))
        inp['b_fc2'] = jnp.zeros((D,), jnp.float32)
        return inp
    _L0_xattn_all = _L0_xattn_setup()
    _L0_xattn_in = {k: v for k, v in _L0_xattn_all.items() if k in ('ln1_scale', 'ln1_offset', 'wq1', 'bq1', 'wk1', 'bk1', 'wv1', 'bv1', 'wo1', 'bo1', 'bias_k1', 'bias_v1', 'ln2_scale', 'ln2_offset', 'wq2', 'bq2', 'wk2', 'bk2', 'wv2', 'bv2', 'wo2', 'bo2', 'bias_k2', 'bias_v2', 'ln_mlp_scale', 'ln_mlp_offset', 'w_fc1', 'b_fc1', 'w_fc2', 'b_fc2')}
    del _L0_xattn_all
    return {'x': x, 'ctx_2048': ctx_2048, 'L0_xattn_ln1_scale': _L0_xattn_in['ln1_scale'], 'L0_xattn_ln1_offset': _L0_xattn_in['ln1_offset'], 'L0_xattn_wq1': _L0_xattn_in['wq1'], 'L0_xattn_bq1': _L0_xattn_in['bq1'], 'L0_xattn_wk1': _L0_xattn_in['wk1'], 'L0_xattn_bk1': _L0_xattn_in['bk1'], 'L0_xattn_wv1': _L0_xattn_in['wv1'], 'L0_xattn_bv1': _L0_xattn_in['bv1'], 'L0_xattn_wo1': _L0_xattn_in['wo1'], 'L0_xattn_bo1': _L0_xattn_in['bo1'], 'L0_xattn_bias_k1': _L0_xattn_in['bias_k1'], 'L0_xattn_bias_v1': _L0_xattn_in['bias_v1'], 'L0_xattn_ln2_scale': _L0_xattn_in['ln2_scale'], 'L0_xattn_ln2_offset': _L0_xattn_in['ln2_offset'], 'L0_xattn_wq2': _L0_xattn_in['wq2'], 'L0_xattn_bq2': _L0_xattn_in['bq2'], 'L0_xattn_wk2': _L0_xattn_in['wk2'], 'L0_xattn_bk2': _L0_xattn_in['bk2'], 'L0_xattn_wv2': _L0_xattn_in['wv2'], 'L0_xattn_bv2': _L0_xattn_in['bv2'], 'L0_xattn_wo2': _L0_xattn_in['wo2'], 'L0_xattn_bo2': _L0_xattn_in['bo2'], 'L0_xattn_bias_k2': _L0_xattn_in['bias_k2'], 'L0_xattn_bias_v2': _L0_xattn_in['bias_v2'], 'L0_xattn_ln_mlp_scale': _L0_xattn_in['ln_mlp_scale'], 'L0_xattn_ln_mlp_offset': _L0_xattn_in['ln_mlp_offset'], 'L0_xattn_w_fc1': _L0_xattn_in['w_fc1'], 'L0_xattn_b_fc1': _L0_xattn_in['b_fc1'], 'L0_xattn_w_fc2': _L0_xattn_in['w_fc2'], 'L0_xattn_b_fc2': _L0_xattn_in['b_fc2']}

def reference(x, ctx_2048, L0_xattn_ln1_scale, L0_xattn_ln1_offset, L0_xattn_wq1, L0_xattn_bq1, L0_xattn_wk1, L0_xattn_bk1, L0_xattn_wv1, L0_xattn_bv1, L0_xattn_wo1, L0_xattn_bo1, L0_xattn_bias_k1, L0_xattn_bias_v1, L0_xattn_ln2_scale, L0_xattn_ln2_offset, L0_xattn_wq2, L0_xattn_bq2, L0_xattn_wk2, L0_xattn_bk2, L0_xattn_wv2, L0_xattn_bv2, L0_xattn_wo2, L0_xattn_bo2, L0_xattn_bias_k2, L0_xattn_bias_v2, L0_xattn_ln_mlp_scale, L0_xattn_ln_mlp_offset, L0_xattn_w_fc1, L0_xattn_b_fc1, L0_xattn_w_fc2, L0_xattn_b_fc2):
    import jax
    import jax.numpy as jnp

    def _L0_xattn_ref(x, xf_1, xf_2, ln1_scale, ln1_offset, wq1, bq1, wk1, bk1, wv1, bv1, wo1, bo1, bias_k1, bias_v1, ln2_scale, ln2_offset, wq2, bq2, wk2, bk2, wv2, bv2, wo2, bo2, bias_k2, bias_v2, ln_mlp_scale, ln_mlp_offset, w_fc1, b_fc1, w_fc2, b_fc2):
        import jax, jax.numpy as jnp
        import numpy as np
        B, Q, S1, S2 = (4, 32, 256, 256)
        D, H, K, F = (256, 16, 128, 1024)
        LN_EPS = 1e-05

        def _layer_norm(x, scale, offset):
            mu = jnp.mean(x, axis=-1, keepdims=True)
            var = jnp.var(x, axis=-1, keepdims=True)
            return (x - mu) * jax.lax.rsqrt(var + LN_EPS) * scale + offset

        def _cross_attention(q_in, kv_in, wq, bq, wk, bk, wv, bv, wo, bo, bias_k, bias_v):
            b, q_len, _ = q_in.shape
            t = kv_in.shape[1]
            qh = (q_in @ wq + bq).reshape(b, q_len, H, K)
            kh = (kv_in @ wk + bk).reshape(b, t, H, K)
            vh = (kv_in @ wv + bv).reshape(b, t, H, K)
            kh = jnp.concatenate([kh, jnp.broadcast_to(bias_k, (b, 1, H, K))], axis=1)
            vh = jnp.concatenate([vh, jnp.broadcast_to(bias_v, (b, 1, H, K))], axis=1)
            scale = jnp.sqrt(jnp.asarray(K, q_in.dtype))
            logits = jnp.einsum('bqhk,bthk->bhqt', qh, kh) / scale
            weights = jax.nn.softmax(logits, axis=-1)
            ctx = jnp.einsum('bhqt,bthk->bqhk', weights, vh).reshape(b, q_len, H * K)
            return ctx @ wo + bo

        def _forward(x, xf_1, xf_2, ln1_scale, ln1_offset, wq1, bq1, wk1, bk1, wv1, bv1, wo1, bo1, bias_k1, bias_v1, ln2_scale, ln2_offset, wq2, bq2, wk2, bk2, wv2, bv2, wo2, bo2, bias_k2, bias_v2, ln_mlp_scale, ln_mlp_offset, w_fc1, b_fc1, w_fc2, b_fc2):
            res = x
            h = _layer_norm(x, ln1_scale, ln1_offset)
            x = res + _cross_attention(h, xf_1, wq1, bq1, wk1, bk1, wv1, bv1, wo1, bo1, bias_k1, bias_v1)
            res = x
            h = _layer_norm(x, ln2_scale, ln2_offset)
            x = res + _cross_attention(h, xf_2, wq2, bq2, wk2, bk2, wv2, bv2, wo2, bo2, bias_k2, bias_v2)
            h = _layer_norm(x, ln_mlp_scale, ln_mlp_offset)
            h = jax.nn.gelu(h @ w_fc1 + b_fc1, approximate=False) @ w_fc2 + b_fc2
            return x + h
        return _forward(x, xf_1, xf_2, ln1_scale, ln1_offset, wq1, bq1, wk1, bk1, wv1, bv1, wo1, bo1, bias_k1, bias_v1, ln2_scale, ln2_offset, wq2, bq2, wk2, bk2, wv2, bv2, wo2, bo2, bias_k2, bias_v2, ln_mlp_scale, ln_mlp_offset, w_fc1, b_fc1, w_fc2, b_fc2)
    x = _L0_xattn_ref(x, ctx_2048, ctx_2048, L0_xattn_ln1_scale, L0_xattn_ln1_offset, L0_xattn_wq1, L0_xattn_bq1, L0_xattn_wk1, L0_xattn_bk1, L0_xattn_wv1, L0_xattn_bv1, L0_xattn_wo1, L0_xattn_bo1, L0_xattn_bias_k1, L0_xattn_bias_v1, L0_xattn_ln2_scale, L0_xattn_ln2_offset, L0_xattn_wq2, L0_xattn_bq2, L0_xattn_wk2, L0_xattn_bk2, L0_xattn_wv2, L0_xattn_bv2, L0_xattn_wo2, L0_xattn_bo2, L0_xattn_bias_k2, L0_xattn_bias_v2, L0_xattn_ln_mlp_scale, L0_xattn_ln_mlp_offset, L0_xattn_w_fc1, L0_xattn_b_fc1, L0_xattn_w_fc2, L0_xattn_b_fc2)
    return x

_drawn_inputs = setup_inputs


def setup_inputs(seed=0):
    import zlib

    import numpy as np

    out = dict(_drawn_inputs(seed))
    spreads = {'L0_xattn_ln1_scale': (1.0, 0.6),
     'L0_xattn_ln1_offset': (0.0, 0.8),
     'L0_xattn_bq1': (0.0, 0.8),
     'L0_xattn_bk1': (0.0, 2.0),
     'L0_xattn_bv1': (0.0, 0.1),
     'L0_xattn_bo1': (0.0, 0.1),
     'L0_xattn_ln2_scale': (1.0, 0.6),
     'L0_xattn_ln2_offset': (0.0, 0.8),
     'L0_xattn_bq2': (0.0, 0.8),
     'L0_xattn_bk2': (0.0, 2.0),
     'L0_xattn_bv2': (0.0, 0.1),
     'L0_xattn_bo2': (0.0, 0.1),
     'L0_xattn_ln_mlp_scale': (1.0, 0.6),
     'L0_xattn_ln_mlp_offset': (0.0, 0.694),
     'L0_xattn_b_fc1': (0.0, 0.1),
     'L0_xattn_b_fc2': (0.0, 0.1)}
    factors = {'L0_xattn_wq1': 8.0,
     'L0_xattn_wk1': 8.0,
     'L0_xattn_bias_k1': 64.0,
     'L0_xattn_bias_v1': 64.0,
     'L0_xattn_wq2': 8.0,
     'L0_xattn_wk2': 8.0,
     'L0_xattn_bias_k2': 64.0,
     'L0_xattn_bias_v2': 64.0}
    for name, (base, spread) in spreads.items():
        noise = np.random.default_rng([zlib.crc32(name.encode()), seed]).standard_normal(out[name].shape)
        drawn = base * np.exp(spread * noise) if base else spread * noise
        out[name] = jnp.asarray(drawn.astype(out[name].dtype))
    for name, factor in factors.items():
        out[name] = (out[name] * factor).astype(out[name].dtype)
    return out
```

```python
import concourse.bass as bass
from concourse import mybir
from contextlib import ExitStack

F32 = mybir.dt.float32
F32R = mybir.dt.float32r
ALU = mybir.AluOpType
ACT = mybir.ActivationFunctionType
X = mybir.AxisListType.X
ds = bass.ds

LAYERS, B, Q, D, H, K, T, F = 2, 8, 56, 256, 16, 128, 1500, 1024
P = 128
DC = D // P
ROWS = B * Q
RG = 4
RGP = ROWS // RG
FLAT = H * Q
TILES = FLAT // P
NT = B * TILES
CT = 125
NCT = T // CT
GRP = 4
NG = NCT // GRP
PIECES = 4
PCT = NCT // PIECES
PT_COLS = T // PIECES
BANK = 512
SPANS = [(0, BANK), (BANK, 2 * BANK), (2 * BANK, T)]
FT = F // P
QUADS = H // 4
JOBS_Q, JOBS_L = H, 2 * H
SCALE = float(K) ** -0.5
LN_EPS = 1e-5
HI, LO = 0, 1
TERMS = ((HI, HI), (HI, LO), (LO, HI))

COL_LN = 0
COL_BQ = COL_LN + 3 * 2 * DC
COL_BV = COL_BQ + LAYERS * H
COL_B1 = COL_BV + LAYERS * H
N_COLS = COL_B1 + FT
INIT = 1
LN_CHAIN = 8
EXTRA = 80


def build(nc, x_rows, ctx_nat, ctx_tr, weights, cols, out_bias, key_rows, head_rows, value_rows,
          ident_in, mask_in, lb_scratch, pb_scratch, out):
    stack = ExitStack()
    with stack:
        place_at = [(nc.sbuf_base + 63) // 64 * 64]

        def sb(name, shape, dtype):
            size = 4
            for n in shape[1:]:
                size *= n
            at = place_at[0]
            place_at[0] += (size + 31) // 32 * 32
            return nc.alloc_sbuf_tensor_at(name, shape, dtype, offset=at)

        def sem(name):
            return stack.enter_context(nc.semaphore(name))

        qt_at = place_at[0]
        qt = sb("qt", [P, DC, B, FLAT], F32)
        nat_stage = sb("nat_stage", [CT, PCT, D], F32)
        tr_stage = sb("tr_stage", [P, DC, PT_COLS], F32)
        qs = sb("qs", [P, 2, DC, P], F32R)
        on = sb("on", [P, D], F32)
        on_lo = sb("on_lo", [P, D], F32)
        xres = sb("xres", [RGP, RG, D], F32)
        w_raw = [sb(f"w_raw{s}", [P, 2 * D], F32) for s in range(2)]
        w = [sb(f"w{s}", [P, 2, 2 * D], F32R) for s in range(2)]
        ident = sb("ident", [P, P], F32)
        col = sb("col", [P, N_COLS], F32)
        bo = sb("bo", [RGP, 3, D], F32)
        lb = sb("lb", [P, NT], F32)
        neg_max = sb("neg_max", [P, NT], F32)
        row_sum = sb("row_sum", [P, NT], F32)
        p_extra = sb("p_extra", [P, NT], F32)
        den = sb("den", [P, NT], F32)
        rden = sb("rden", [P, NT], F32)
        pn_extra = sb("pn_extra", [P, NT], F32)
        mx = sb("mx", [P, 4], F32)
        g_cols = sb("g_cols", [P, DC, H], F32)
        cq = sb("cq", [H, LAYERS], F32)
        dv = sb("dv", [EXTRA, LAYERS, K], F32)
        mask = sb("mask", [EXTRA, H], F32)
        p80_raw = sb("p80_raw", [EXTRA, B, Q], F32)
        ln_stat = sb("ln_stat", [RGP, RG, 6], F32)
        ln_mv = sb("ln_mv", [RGP, RG, 2], F32)
        ln_v = sb("ln_v", [RGP, RG], F32)
        ln_s = sb("ln_s", [RGP, RG], F32)
        ln_y = sb("ln_y", [RGP, RG], F32)
        ln_t = sb("ln_t", [RGP, RG], F32)
        ln_u = sb("ln_u", [RGP, RG], F32)
        ln_r = sb("ln_r", [RGP, RG], F32)

        exp_at = place_at[0]
        e = sb("e", [P, T + 4], F32)
        pt = sb("pt", [CT, 2, NG, GRP * P], F32R)
        after_exp = place_at[0]
        place_at[0] = exp_at
        key_row = sb("key_row", [1, 2, H * K], F32)
        assert place_at[0] <= after_exp
        place_at[0] = after_exp

        N_TR, N_NAT = DC * 2 * T, NCT * 2 * D
        slot_words = N_TR + N_NAT
        ctx = sb("ctx", [P, 2, slot_words], F32R)
        end = place_at[0]
        assert end <= nc.sbuf_usable_end, (end, nc.sbuf_usable_end)

        scratch_at = end - slot_words * 4
        place_at[0] = scratch_at
        xn = sb("xn", [RGP, RG, D], F32)
        ht32 = sb("ht32", [P, DC, ROWS], F32)
        ht = sb("ht", [P, 2, DC, ROWS], F32R)
        after_ln = place_at[0]
        qh = [sb(f"qh{s}", [P, 2, ROWS], F32R) for s in range(2)]
        dk_all = sb("dk_all", [P, H * K], F32)
        g_prod = [sb(f"g_prod{s}", [P, DC, K], F32) for s in range(2)]
        lb_rows = sb("lb_rows", [H, B, Q], F32)
        lb_tiles = sb("lb_tiles", [NT, P], F32)
        assert place_at[0] <= end
        place_at[0] = after_ln
        cs = [sb(f"cs{s}", [P, 2, ROWS], F32R) for s in range(2)]
        y_lo = [sb(f"y_lo{s}", [RGP, D], F32) for s in range(2)]
        pm = [sb(f"pm{s}", [EXTRA, ROWS], F32R) for s in range(2)]
        p80 = sb("p80", [EXTRA, ROWS], F32R)
        dv80 = sb("dv80", [EXTRA, K], F32R)
        pb_tiles = sb("pb_tiles", [NT, P], F32)
        oth_at = place_at[0]
        oth = [sb(f"oth{s}", [P, 2, DC, ROWS], F32R) for s in range(2)]
        assert place_at[0] <= end
        place_at[0] = oth_at
        g32 = [sb(f"g32_{s}", [P, ROWS], F32) for s in range(2)]
        assert place_at[0] <= end
        place_at[0] = qt_at
        hrow = sb("hrow", [H, 3, LAYERS, K], F32)
        vrow = sb("vrow", [EXTRA, 2, LAYERS, K], F32)
        hprod = sb("hprod", [H, LAYERS, K], F32)

        logits = stack.enter_context(nc.psum_tensor("logits", [P, 3 * BANK], F32))
        single = [stack.enter_context(nc.psum_tensor(f"bank{i}", [P, BANK], F32)) for i in range(3, 8)]
        bank = [logits[:, i * BANK:(i + 1) * BANK] for i in range(3)] + [t[:, :] for t in single]
        TP = [bank[3], bank[4], bank[7]]
        O_BANK, OT_BANK = bank[5], bank[6]
        LN_BANK = [bank[6], bank[7]]
        Q_BANK = [bank[3], bank[4]]
        QP_BANK = [[bank[5], bank[6]], [bank[0], bank[1]]]
        C_BANK = [bank[3], bank[4]]
        Y_BANK = [bank[0], bank[1], bank[2], bank[5]]

        zeroed = sem("zeroed")
        consts_in = sem("consts_in")
        setup_step = sem("setup_step")
        cq_ready = sem("cq_ready")
        nat_in, tr_in = sem("nat_in"), sem("tr_in")
        ctx_hi, ctx_lo = sem("ctx_hi"), sem("ctx_lo")
        w_in = [sem(f"w_in{s}") for s in range(2)]
        w_hi = [sem(f"w_hi{s}") for s in range(2)]
        w_lo = [sem(f"w_lo{s}") for s in range(2)]
        w_used = [sem(f"w_used{s}") for s in range(2)]
        krow_in, dk_step = sem("krow_in"), sem("dk_step")
        gp_ready = [sem(f"gp_ready{s}") for s in range(2)]
        gp_used = [sem(f"gp_used{s}") for s in range(2)]
        ln_stats, ln_aggr, ln_chain, ln_sqrt = sem("ln_stats"), sem("ln_aggr"), sem("ln_chain"), sem("ln_sqrt")
        xn_ready, xt_mm = sem("xn_ready"), sem("xt_mm")
        h32_ready, h_hi, h_lo = sem("h32_ready"), sem("h_hi"), sem("h_lo")
        q_mm = [sem(f"q_mm{s}") for s in range(2)]
        q_hi = [sem(f"q_hi{s}") for s in range(2)]
        q_lo = [sem(f"q_lo{s}") for s in range(2)]
        qp_mm = [sem(f"qp_mm{s}") for s in range(2)]
        qp_out0 = [sem(f"qp_out0_{s}") for s in range(2)]
        qp_out1 = [sem(f"qp_out1_{s}") for s in range(2)]
        lb_mm, lb_rows_ready, lb_written, lb_in, lb_tr, lb_ready = (
            sem("lb_mm"), sem("lb_rows_ready"), sem("lb_written"), sem("lb_in"), sem("lb_tr"), sem("lb_ready"))
        qs_hi, qs_lo = sem("qs_hi"), sem("qs_lo")
        s_mm = sem("s_mm")
        mx_step, max_ready = sem("mx_step"), sem("max_ready")
        exp_done, pe_done = sem("exp_done"), sem("pe_done")
        den_ready, rden_ready, pn_ready = sem("den_ready"), sem("rden_ready"), sem("pn_ready")
        tp_mm, pt_hi, pt_lo = sem("tp_mm"), sem("pt_hi"), sem("pt_lo")
        pv_mm, onlo_ready, on_ready = sem("pv_mm"), sem("onlo_ready"), sem("on_ready")
        ot_mm, ot_out = sem("ot_mm"), sem("ot_out")
        pb_tr, pb_ready, pb_written, pb_in = sem("pb_tr"), sem("pb_ready"), sem("pb_written"), sem("pb_in")
        x80_step = sem("x80_step")
        pm_ready = [sem(f"pm_ready{s}") for s in range(2)]
        oth_hi = [sem(f"oth_hi{s}") for s in range(2)]
        oth_lo = [sem(f"oth_lo{s}") for s in range(2)]
        c_mm = [sem(f"c_mm{s}") for s in range(2)]
        c_hi = [sem(f"c_hi{s}") for s in range(2)]
        c_lo = [sem(f"c_lo{s}") for s in range(2)]
        g32_ready = [sem(f"g32_ready{s}") for s in range(2)]
        xb_ready, ylo_ready, xs_ready, x_ready = sem("xb_ready"), sem("ylo_ready"), sem("xs_ready"), sem("x_ready")
        out_written = sem("out_written")
        settled = sem("settled")

        N_CONSTS = 9

        def settle(eng):
            eng.sem_inc(settled, 1)

        started_by = {
            "pe": [*w_used, xt_mm, *q_mm, *qp_mm, lb_mm, lb_tr, s_mm, tp_mm, pv_mm, ot_mm, pb_tr, *c_mm],
            "act": [ln_sqrt, h_hi, *q_hi, *qp_out0, exp_done, pe_done, pt_hi, onlo_ready, ot_out, *oth_hi,
                    *c_hi, *g32_ready, ylo_ready],
            "dve": [x_ready, ln_stats, ln_aggr, ln_chain, xn_ready, h32_ready, h_lo, cq_ready, *gp_used, *q_lo,
                    *qp_out1, lb_rows_ready, lb_ready, mx_step, max_ready, den_ready, rden_ready, pn_ready,
                    pt_lo, on_ready, pb_ready, *oth_lo, *c_lo, xb_ready, xs_ready],
            "pool": [zeroed, setup_step, ctx_hi, ctx_lo, *w_hi, *w_lo, dk_step, *gp_ready, qs_hi, qs_lo,
                     x80_step, *pm_ready],
        }

        def start(eng, name):
            for counter in started_by[name]:
                eng.sem_inc(counter, INIT)

        qt_flat = qt[:].rearrange("p c b f -> p c (b f)")

        def head_rows_of(h):
            return qt[:, :, :, ds(h * Q, Q)]

        def ctx_tr_part(slot, half, part, lo, hi):
            at = (half * 2 + part) * T
            return ctx[:, ds(slot, 1), at + lo:at + hi].rearrange("p a t -> p (a t)")

        def ctx_nat_tile(slot, t, width):
            at = N_TR + t * 2 * D
            return ctx[0:CT, ds(slot, 1), at:at + width].rearrange("p a t -> p (a t)")

        def as_f32(ap):
            return ap.bitcast(F32)

        def batch_qrows(ap):
            return ap.rearrange("p (b q) -> p b q", b=B)

        block = stack.enter_context(nc.Block())

        @block.sync
        def _(sp):
            def load_weight(job, s, n):
                sp.wait_ge(w_lo[s], INIT + n)
                sp.dma_start(w_raw[s][:], weights[ds(job, 1)].rearrange("a p n -> (a p) n")).then_inc(w_in[s], 16)

            def load_piece(batch, n, p):
                sp.wait_ge(ctx_lo, INIT + 2 * n)
                sp.dma_start(nat_stage[:], ctx_nat[ds(batch, 1), ds(p, 1)].rearrange(
                    "a b t c d -> (a b t) c d")).then_inc(nat_in, 16)
                sp.dma_start(tr_stage[:], ctx_tr[ds(batch, 1), ds(p, 1)].rearrange(
                    "a b p c t -> (a b p) c t")).then_inc(tr_in, 16)

            sp.dma_start(xres[:], x_rows).then_inc(consts_in, 16)
            sp.dma_start(col[:], cols).then_inc(consts_in, 16)
            sp.dma_start(ident[:], ident_in).then_inc(consts_in, 16)
            sp.dma_start(bo[:], out_bias.partition_broadcast(RGP)).then_inc(consts_in, 16)
            sp.dma_start(hrow[:], head_rows).then_inc(consts_in, 16)
            sp.dma_start(mask[:], mask_in).then_inc(consts_in, 16)
            sp.wait_ge(zeroed, INIT + 2)
            for g in range(3):
                sp.dma_start(vrow[32 * g:32 * g + H], value_rows).then_inc(consts_in, 16)

            with sp.Fori(0, LAYERS) as l:
                sp.wait_ge(pv_mm, INIT + l * NT)
                sp.dma_start(key_row[:], key_rows[ds(l, 1)]).then_inc(krow_in, 16)
                with sp.Fori(0, QUADS) as quad:
                    for u in range(4):
                        s, n = u % 2, quad * 2 + u // 2
                        sp.wait_ge(gp_ready[s], INIT + l * 8 + n)
                        load_weight(l * JOBS_L + quad * 4 + u, s, l * 16 + n)
                    load_piece(0, l * (B * PIECES) + quad, quad)

                sp.wait_ge(lb_rows_ready, INIT + l + 1)
                sp.dma_start(lb_scratch.rearrange("(b h q) -> h b q", b=B, h=H), lb_rows[:]).then_inc(lb_written, 16)
                sp.wait_ge(lb_written, (l + 1) * 16)
                sp.dma_start(lb_tiles[:], lb_scratch.rearrange("(t p) -> t p", p=P)).then_inc(lb_in, 16)

                with sp.Fori(0, B - 1) as b:
                    for p in range(PIECES):
                        load_piece(b + 1, l * (B * PIECES) + b * PIECES + PIECES + p, p)

                first_out = l * JOBS_L + JOBS_Q
                for s in range(2):
                    sp.wait_ge(gp_ready[s], INIT + l * 8 + 8)
                    load_weight(first_out + s, s, l * 16 + 8)
                sp.wait_ge(pb_ready, INIT + l + 1)
                sp.dma_start(pb_scratch.rearrange("(t p) -> t p", p=P), pb_tiles[:]).then_inc(pb_written, 16)
                sp.wait_ge(pb_written, (l + 1) * 16)
                for g in range(3):
                    sp.dma_start(p80_raw[32 * g:32 * g + H], pb_scratch.rearrange(
                        "(b h q) -> h b q", b=B, h=H)).then_inc(pb_in, 16)
                with sp.Fori(0, QUADS - 1) as quad:
                    for u in range(4):
                        load_weight(first_out + 2 + quad * 4 + u, u % 2, l * 16 + 9 + quad * 2 + u // 2)
                for s in range(2):
                    load_weight(first_out + H - 2 + s, s, l * 16 + 15)

            with sp.Fori(0, FT // 4) as quad:
                for u in range(4):
                    load_weight(LAYERS * JOBS_L + quad * 4 + u, u % 2, LAYERS * 16 + quad * 2 + u // 2)

            sp.wait_ge(x_ready, INIT + 3 * RG)
            sp.dma_start(out, xres[:]).then_inc(out_written, 16)
            sp.wait_ge(out_written, 16)

        @block.gpsimd
        def _(pool):
            def split_weight(s, n):
                pool.wait_ge(w_in[s], (n + 1) * 16)
                pool.wait_ge(w_used[s], INIT + n)
                settle(pool)
                nc.gpsimd.tensor_copy(w[s][:, HI, :], w_raw[s][:]).then_inc(w_hi[s], 1)
                pool.wait_ge(w_hi[s], INIT + n + 1)
                settle(pool)
                nc.gpsimd.tensor_tensor(w[s][:, LO, :], w_raw[s][:], as_f32(w[s][:, HI, :]),
                                        ALU.subtract).then_inc(w_lo[s], 1)

            def split_piece(slot, n, p):
                at = p * (PCT * 2 * D)
                nat = ctx[0:CT, ds(slot, 1), ds(at + N_TR, PCT * 2 * D)].rearrange(
                    "p a (t c d) -> p (a t) c d", t=PCT, c=2)
                tr = ctx[:, ds(slot, 1), 0:N_TR].rearrange("p a (c h t) -> p (a c) h t", c=DC, h=2)
                tr = tr[:, :, :, ds(p * PT_COLS, PT_COLS)]
                pool.wait_ge(nat_in, n * 16 + 16)
                settle(pool)
                nc.gpsimd.tensor_copy(nat[:, :, HI, :], nat_stage[:]).then_inc(ctx_hi, 1)
                pool.wait_ge(tr_in, n * 16 + 16)
                settle(pool)
                nc.gpsimd.tensor_copy(tr[:, :, HI, :], tr_stage[:]).then_inc(ctx_hi, 1)
                pool.wait_ge(ctx_hi, INIT + n * 2 + 2)
                settle(pool)
                nc.gpsimd.tensor_tensor(nat[:, :, LO, :], nat_stage[:], as_f32(nat[:, :, HI, :]),
                                        ALU.subtract).then_inc(ctx_lo, 1)
                nc.gpsimd.tensor_tensor(tr[:, :, LO, :], tr_stage[:], as_f32(tr[:, :, HI, :]),
                                        ALU.subtract).then_inc(ctx_lo, 1)

            def split_q(tile, n):
                src = qt_flat[:, :, ds(tile * P, P)]
                nc.gpsimd.tensor_copy(qs[:, HI], src).then_inc(qs_hi, 1)
                pool.wait_ge(qs_hi, INIT + n + 1)
                settle(pool)
                nc.gpsimd.tensor_tensor(qs[:, LO], src, as_f32(qs[:, HI]), ALU.subtract).then_inc(qs_lo, 1)

            start(pool, "pool")
            nc.gpsimd.memset(vrow[:], 0.0).then_inc(zeroed, 1)
            nc.gpsimd.memset(p80_raw[:], 0.0).then_inc(zeroed, 1)
            pool.wait_ge(consts_in, 16 * N_CONSTS)
            nc.gpsimd.tensor_tensor(dv[:], vrow[:, 0], vrow[:, 1], ALU.subtract).then_inc(setup_step, 1)
            nc.gpsimd.tensor_tensor(hprod[:], hrow[:, 0], hrow[:, 1], ALU.subtract).then_inc(setup_step, 1)
            pool.wait_ge(setup_step, INIT + 2)
            settle(pool)
            nc.gpsimd.tensor_tensor(hprod[:], hprod[:], hrow[:, 2], ALU.mult).then_inc(setup_step, 1)

            with pool.Fori(0, LAYERS) as l:
                pool.wait_ge(krow_in, l * 16 + 16)
                settle(pool)
                nc.gpsimd.tensor_tensor(key_row[:, 0], key_row[:, 0], key_row[:, 1],
                                        ALU.subtract).then_inc(dk_step, 1)
                pool.wait_ge(dk_step, INIT + l * 2 + 1)
                pool.wait_ge(x_ready, INIT + l * RG)
                settle(pool)
                nc.gpsimd.partition_broadcast(dk_all[:], key_row[:, 0], channels=P).then_inc(dk_step, 1)
                pool.wait_ge(dk_step, INIT + l * 2 + 2)
                settle(pool)
                with pool.Fori(0, QUADS) as quad:
                    for u in range(4):
                        s, n = u % 2, quad * 2 + u // 2
                        split_weight(s, l * 16 + n)
                        pool.wait_ge(gp_used[s], INIT + l * 8 + n)
                        settle(pool)
                        nc.gpsimd.tensor_tensor(
                            g_prod[s][:], w_raw[s][:, 0:DC * K].rearrange("p (c k) -> p c k", c=DC),
                            dk_all[:, ds(quad * (4 * K) + u * K, K)].rearrange("p (a k) -> p a k", a=1)
                            .to_broadcast([P, DC, K]), ALU.mult).then_inc(gp_ready[s], 1)
                    split_piece(0, l * (B * PIECES) + quad, quad)

                for s in range(2):
                    pool.wait_ge(qp_out0[s], INIT + l * 8 + 8)
                    pool.wait_ge(qp_out1[s], INIT + l * 8 + 8)
                    settle(pool)
                split_q(0, l * NT)
                pool.wait_ge(s_mm, INIT + (l * NT + 1) * 3)
                settle(pool)
                split_q(1, l * NT + 1)
                pool.wait_ge(lb_ready, INIT + l + 1)
                settle(pool)

                def next_q(tile):
                    pool.wait_ge(s_mm, INIT + (l * NT + tile + 2) * 3)
                    settle(pool)
                    split_q(tile + 2, l * NT + tile + 2)

                next_q(0)
                with pool.Fori(0, B - 1) as b:
                    pool.wait_ge(pv_mm, INIT + l * NT + b * TILES)
                    settle(pool)
                    for r in range(1, TILES + 1):
                        next_q(b * TILES + r)
                        if r <= PIECES:
                            split_piece((b + 1) & 1, l * (B * PIECES) + b * PIECES + PIECES + r - 1, r - 1)
                for tile in range(NT - TILES + 1, NT - 2):
                    next_q(tile)

                for s in range(2):
                    split_weight(s, l * 16 + 8)
                pool.wait_ge(pv_mm, INIT + (l + 1) * NT)
                settle(pool)
                dv_l = dv[:, ds(l, 1), :].rearrange("p a k -> p (a k)")
                nc.gpsimd.tensor_copy(dv80[:], dv_l).then_inc(x80_step, 1)
                pool.wait_ge(x80_step, INIT + l * 4 + 1)
                settle(pool)
                nc.gpsimd.tensor_tensor(dv80[32:64], dv_l[32:64], as_f32(dv80[32:64]),
                                        ALU.subtract).then_inc(x80_step, 1)
                pool.wait_ge(pb_in, l * 48 + 48)
                settle(pool)
                pool.wait_ge(x80_step, INIT + l * 4 + 2)
                settle(pool)
                raw = p80_raw[:].rearrange("p b q -> p (b q)")
                nc.gpsimd.tensor_copy(p80[:], raw).then_inc(x80_step, 1)
                pool.wait_ge(x80_step, INIT + l * 4 + 3)
                settle(pool)
                nc.gpsimd.tensor_tensor(p80[64:EXTRA], raw[64:EXTRA], as_f32(p80[64:EXTRA]),
                                        ALU.subtract).then_inc(x80_step, 1)
                pool.wait_ge(x80_step, INIT + l * 4 + 4)
                settle(pool)

                def mask_extra(h, s, n):
                    pool.wait_ge(c_mm[s], INIT + n)
                    settle(pool)
                    nc.gpsimd.tensor_tensor(pm[s][:], as_f32(p80[:]), mask[:, ds(h, 1)].to_broadcast([EXTRA, ROWS]),
                                            ALU.mult).then_inc(pm_ready[s], 1)

                for s in range(2):
                    mask_extra(s, s, l * 8)
                with pool.Fori(0, QUADS - 1) as quad:
                    for u in range(4):
                        n = quad * 2 + u // 2 + 1
                        split_weight(u % 2, l * 16 + 8 + n)
                        mask_extra(quad * 4 + u + 2, u % 2, l * 8 + n)
                for s in range(2):
                    split_weight(s, l * 16 + 15)
                    mask_extra(H - 2 + s, s, l * 8 + 7)

            with pool.Fori(0, FT // 4) as quad:
                for u in range(4):
                    split_weight(u % 2, LAYERS * 16 + quad * 2 + u // 2)

        @block.tensor
        def _(pe):
            mm = nc.tensor.matmul

            def norm_transposes(m):
                pe.wait_ge(xn_ready, INIT + m * RG + RG)
                for c in range(DC):
                    for g in range(RG):
                        last = nc.tensor.transpose(LN_BANK[c][:, g * RGP:(g + 1) * RGP],
                                                   xn[:, g, c * P:(c + 1) * P], ident[0:RGP, 0:RGP])
                    last.then_inc(xt_mm, 1)

            def project(out_bank, s, moving, more):
                for c in range(DC):
                    for a, m in TERMS:
                        last = mm(out_bank, w[s][:, a, c * P:(c + 1) * P], moving(m, c),
                                  start=(c == 0 and (a, m) == (HI, HI)),
                                  stop=(not more and c == DC - 1 and (a, m) == (LO, HI)))
                return last

            def queries(s, n, job):
                pe.wait_ge(w_lo[s], INIT + job + 1)
                pe.wait_ge(q_lo[s], INIT + n)
                project(Q_BANK[s][:, 0:ROWS], s, lambda m, c: ht[:, m, c, :], False).then_inc(q_mm[s], 1)

            def carried_queries(s, n):
                pe.wait_ge(q_lo[s], INIT + n + 1)
                pe.wait_ge(qp_out0[s], INIT + n)
                pe.wait_ge(qp_out1[s], INIT + n)
                for c in range(DC):
                    for a, m in TERMS:
                        last = mm(QP_BANK[s][c][:, 0:ROWS], w[s][:, a, D + c * P:D + (c + 1) * P], qh[s][:, m, :],
                                  start=(a, m) == (HI, HI), stop=(a, m) == (LO, HI))
                    last.then_inc(qp_mm[s] if c == 0 else w_used[s], 1)

            def exp_transposes(g, n):
                for j in range(GRP):
                    t = g * GRP + j
                    last = nc.tensor.transpose(TP[g][0:CT, j * P:(j + 1) * P], e[:, t * CT:(t + 1) * CT], ident[:])
                last.then_inc(tp_mm, 1)

            def logit_bank(k, slot):
                lo, hi = SPANS[k]
                terms = [(c, a, m) for c in range(DC) for a, m in TERMS]
                for c, a, m in terms:
                    last = mm(logits[:, lo:hi], qs[:, a, c, :], ctx_tr_part(slot, c, m, lo, hi),
                              start=(c, a, m) == terms[0], stop=(c, a, m) == terms[-1])
                last.then_inc(s_mm, 1)

            def weighted_context(slot, n):
                pe.wait_ge(on_ready, INIT + n)
                for g in range(NG):
                    pe.wait_ge(pt_lo, INIT + n * NG + g + 1)
                    for j in range(GRP):
                        t = g * GRP + j
                        mm(O_BANK[:, 0:2 * D], pt[:, HI, g, j * P:(j + 1) * P], ctx_nat_tile(slot, t, 2 * D),
                           start=(t == 0), stop=(t == NCT - 1), skip_group_check=True)
                        last = mm(O_BANK[:, 0:D], pt[:, LO, g, j * P:(j + 1) * P], ctx_nat_tile(slot, t, D),
                                  start=False, stop=(t == NCT - 1), skip_group_check=True)
                last.then_inc(pv_mm, 1)

            def context_transposes(n):
                pe.wait_ge(on_ready, INIT + n + 1)
                pe.wait_ge(ot_out, INIT + n)
                for c in range(DC):
                    last = nc.tensor.transpose(OT_BANK[:, c * P:(c + 1) * P], on[:, c * P:(c + 1) * P], ident[:])
                last.then_inc(ot_mm, 1)

            def head_context(s, n, job, extra):
                pe.wait_ge(w_lo[s], INIT + job + 1)
                pe.wait_ge(c_lo[s], INIT + n)
                if extra:
                    pe.wait_ge(oth_lo[s], INIT + n + 1)
                    pe.wait_ge(pm_ready[s], INIT + n + 1)
                    project(C_BANK[s][:, 0:ROWS], s, lambda m, c: oth[s][:, m, c, :], True)
                    mm(C_BANK[s][:, 0:ROWS], dv80[:], pm[s][:], start=False, stop=True).then_inc(c_mm[s], 1)
                else:
                    project(C_BANK[s][:, 0:ROWS], s, lambda m, c: ht[:, m, c, :], False).then_inc(c_mm[s], 1)

            def output_rows(s, n, first, last_head):
                pe.wait_ge(c_lo[s], INIT + n + 1)
                for g in range(RG):
                    rows = slice(g * RGP, (g + 1) * RGP)
                    mm(Y_BANK[g][0:RGP, 0:2 * D], cs[s][:, HI, rows], w[s][:, :, D:2 * D],
                       start=first, stop=last_head, skip_group_check=True)
                    last = mm(Y_BANK[g][0:RGP, 0:D], cs[s][:, LO, rows], w[s][:, HI, D:2 * D],
                              start=False, stop=last_head, skip_group_check=True)
                last.then_inc(w_used[s], 1)

            def output_quad(n, job, extra, first, last_quad):
                for pair in range(2):
                    for s in range(2):
                        head_context(s, n + pair, job + pair, extra)
                    for s in range(2):
                        output_rows(s, n + pair, first and pair == 0 and s == 0, last_quad and pair == 1 and s == 1)

            start(pe, "pe")
            pe.wait_ge(consts_in, 16 * N_CONSTS)
            with pe.Fori(0, LAYERS) as l:
                norm_transposes(l)
                pe.wait_ge(h_lo, INIT + l * DC + DC)
                settle(pe)
                with pe.Fori(0, QUADS) as quad:
                    for pair in range(2):
                        for s in range(2):
                            queries(s, l * 8 + quad * 2 + pair, l * 16 + quad * 2 + pair)
                        for s in range(2):
                            carried_queries(s, l * 8 + quad * 2 + pair)
                for s in range(2):
                    pe.wait_ge(gp_used[s], INIT + l * 8 + 8)
                for c in range(DC):
                    last = mm(bank[7][0:H, 0:ROWS], g_cols[:, c, :], ht32[:, c, :], start=(c == 0), stop=(c == DC - 1))
                last.then_inc(lb_mm, 1)

                tiles = l * NT
                pe.wait_ge(qs_lo, INIT + tiles + 1)
                pe.wait_ge(ctx_lo, INIT + l * (2 * B * PIECES) + 2 * PIECES)
                for k in range(3):
                    logit_bank(k, 0)
                pe.wait_ge(lb_in, l * 16 + 16)
                settle(pe)
                nc.tensor.transpose(bank[6][:, 0:NT], lb_tiles[:], ident[0:NT, 0:NT]).then_inc(lb_tr, 1)

                def row_tile(tile, slot, next_slot, new_batch, has_next, has_before):
                    n = tiles + tile
                    pe.wait_ge(exp_done, INIT + n + 1)
                    pe.wait_ge(pt_lo, INIT + n * NG)
                    if has_next:
                        pe.wait_ge(qs_lo, INIT + n + 2)
                    if new_batch is not None:
                        pe.wait_ge(ctx_lo, INIT + l * (2 * B * PIECES) + new_batch * (2 * PIECES) + 2 * PIECES)
                    for k in range(NG):
                        exp_transposes(k, n)
                        if has_next:
                            logit_bank(k, next_slot)
                        if has_before and k == 0:
                            context_transposes(n - 1)
                    weighted_context(slot, n)

                row_tile(0, 0, 0, None, True, False)
                with pe.Fori(0, B - 1) as b:
                    for r in range(1, TILES + 1):
                        row_tile(b * TILES + r, (b + r // TILES) & 1, (b + (r + 1) // TILES) & 1,
                                 b + 1 if r == TILES - 1 else None, True, True)
                for r in range(1, TILES):
                    row_tile((B - 1) * TILES + r, (B - 1) & 1, (B - 1) & 1, None, r < TILES - 1, True)
                context_transposes(tiles + NT - 1)
                pe.wait_ge(pn_ready, INIT + tiles + NT)
                settle(pe)
                nc.tensor.transpose(bank[7][0:NT, 0:P], pn_extra[:], ident[:]).then_inc(pb_tr, 1)

                output_quad(l * 8, l * 16 + 8, True, True, False)
                with pe.Fori(1, QUADS - 1) as quad:
                    output_quad(l * 8 + quad * 2, l * 16 + quad * 2 + 8, True, False, False)
                output_quad(l * 8 + 6, l * 16 + 14, True, False, True)

            norm_transposes(LAYERS)
            pe.wait_ge(h_lo, INIT + LAYERS * DC + DC)
            output_quad(LAYERS * 8, LAYERS * 16, False, True, False)
            output_quad(LAYERS * 8 + 2, LAYERS * 16 + 2, False, False, True)

        @block.scalar
        def _(act):
            go = nc.scalar.activation

            def norm(m):
                act.wait_ge(ln_chain, INIT + m * LN_CHAIN + 1)
                go(ln_s[:], ln_v[:], ACT.Sqrt).then_inc(ln_sqrt, 1)
                for c in range(DC):
                    act.wait_ge(h32_ready, INIT + m * DC + c + 1)
                    go(ht[:, HI, c, :], ht32[:, c, :], ACT.Copy).then_inc(h_hi, 1)

            def exponentials(tile, n):
                at = ds(tile, 1)
                act.wait_ge(max_ready, INIT + n + 1)
                go(e[:, 0:T], logits[:, 0:T], ACT.Exp, bias=neg_max[:, at],
                   accum_out=row_sum[:, at]).then_inc(exp_done, 1)
                go(p_extra[:, at], lb[:, at], ACT.Exp, bias=neg_max[:, at]).then_inc(pe_done, 1)

            def transposed_context(tile, n):
                act.wait_ge(ot_mm, INIT + n + 1)
                go(qt_flat[:, :, ds(tile * P, P)], OT_BANK[:, 0:D].rearrange("p (c r) -> p c r", c=DC),
                   ACT.Copy).then_inc(ot_out, 1)

            def output_sum(m):
                for g in range(RG):
                    if g >= 2:
                        act.wait_ge(x_ready, INIT + m * RG + g - 1)
                    go(y_lo[g % 2][:], Y_BANK[g][0:RGP, D:2 * D], ACT.Copy).then_inc(ylo_ready, 1)

            start(act, "act")
            with act.Fori(0, LAYERS) as l:
                norm(l)
                with act.Fori(0, QUADS) as quad:
                    for pair in range(2):
                        n = l * 8 + quad * 2 + pair
                        for s in range(2):
                            act.wait_ge(q_mm[s], INIT + n + 1)
                            act.wait_ge(w_used[s], INIT + l * 16 + quad * 2 + pair)
                            go(qh[s][:, HI, :], Q_BANK[s][:, 0:ROWS], ACT.Identity,
                               bias=col[:, ds(l * H + quad * 4 + (COL_BQ + pair * 2 + s), 1)]).then_inc(q_hi[s], 1)
                        for s in range(2):
                            act.wait_ge(qp_mm[s], INIT + n + 1)
                            go(head_rows_of(quad * 4 + (pair * 2 + s))[:, 0], batch_qrows(QP_BANK[s][0][:, 0:ROWS]),
                               ACT.Copy, scale=SCALE).then_inc(qp_out0[s], 1)

                tiles = l * NT
                act.wait_ge(lb_ready, INIT + l + 1)
                exponentials(0, tiles)

                def row_tile(tile, has_next, has_before):
                    n = tiles + tile
                    for g in range(NG):
                        act.wait_ge(tp_mm, INIT + n * NG + g + 1)
                        go(pt[:, HI, g, :], TP[g][0:CT, :], ACT.Copy).then_inc(pt_hi, 1)
                        if g == 1 and has_before:
                            transposed_context(tile - 1, n - 1)
                    if has_next:
                        exponentials(tile + 1, n + 1)
                    act.wait_ge(pv_mm, INIT + n + 1)
                    act.wait_ge(rden_ready, INIT + n + 1)
                    act.wait_ge(on_ready, INIT + n)
                    go(on_lo[:], O_BANK[:, D:2 * D], ACT.Copy, scale=rden[:, ds(tile, 1)]).then_inc(onlo_ready, 1)

                row_tile(0, True, False)
                with act.Fori(0, B - 1) as b:
                    for r in range(1, TILES + 1):
                        row_tile(b * TILES + r, True, True)
                for r in range(1, TILES):
                    row_tile((B - 1) * TILES + r, r < TILES - 1, True)
                transposed_context(NT - 1, tiles + NT - 1)
                act.wait_ge(ot_out, INIT + tiles + NT)

                def split_hi(h, s, n):
                    act.wait_ge(c_mm[s], INIT + n)
                    go(oth[s][:, HI].rearrange("p c (b q) -> p c b q", b=B), head_rows_of(h),
                       ACT.Copy).then_inc(oth_hi[s], 1)

                def heads(quad_h, n, job, last_quad):
                    for u in range(4):
                        s, k = u % 2, u // 2
                        act.wait_ge(c_mm[s], INIT + n + k + 1)
                        act.wait_ge(w_used[s], INIT + job + k)
                        go(cs[s][:, HI, :], C_BANK[s][:, 0:ROWS], ACT.Identity,
                           bias=col[:, ds(l * H + quad_h + (COL_BV + u), 1)]).then_inc(c_hi[s], 1)
                        if not (last_quad and k == 1):
                            split_hi(quad_h + (u + 2), s, n + k + 1)

                for s in range(2):
                    split_hi(s, s, l * 8)
                with act.Fori(0, QUADS - 1) as quad:
                    heads(quad * 4, l * 8 + quad * 2, l * 16 + quad * 2 + 8, False)
                heads(4 * (QUADS - 1), l * 8 + 6, l * 16 + 14, True)
                for s in range(2):
                    act.wait_ge(w_used[s], INIT + l * 16 + 16)
                output_sum(l)

            norm(LAYERS)
            with act.Fori(0, FT // 4) as quad:
                for pair in range(2):
                    n = quad * 2 + (16 + pair)
                    for s in range(2):
                        act.wait_ge(c_mm[s], INIT + n + 1)
                        act.wait_ge(c_lo[s], INIT + n)
                        go(g32[s][:], C_BANK[s][:, 0:ROWS], ACT.Gelu,
                           bias=col[:, ds(quad * 4 + (COL_B1 + pair * 2 + s), 1)]).then_inc(g32_ready[s], 1)
                    for s in range(2):
                        act.wait_ge(g32_ready[s], INIT + quad * 2 + (pair + 1))
                        act.wait_ge(w_used[s], INIT + quad * 2 + (LAYERS * 16 + pair))
                        go(cs[s][:, HI, :], g32[s][:], ACT.Copy).then_inc(c_hi[s], 1)
            for s in range(2):
                act.wait_ge(w_used[s], INIT + LAYERS * 16 + FT // 2)
            output_sum(LAYERS)

        @block.vector
        def _(dve):
            V = nc.vector

            def norm(m):
                base = m * LN_CHAIN
                dve.wait_ge(x_ready, INIT + m * RG)
                for g in range(RG):
                    V.bn_stats(ln_stat[:, g, :], xres[:, g, :]).then_inc(ln_stats, 1)
                for g in range(RG):
                    dve.wait_ge(ln_stats, INIT + m * RG + g + 1)
                    settle(dve)
                    V.bn_aggr(ln_mv[:, g, :], ln_stat[:, g, :]).then_inc(ln_aggr, 1)
                dve.wait_ge(ln_aggr, INIT + m * RG + RG)
                V.tensor_scalar(ln_v[:], ln_mv[:, :, 1], LN_EPS, None, ALU.add).then_inc(ln_chain, 1)
                dve.wait_ge(ln_sqrt, INIT + m + 1)
                V.reciprocal(ln_y[:], ln_s[:]).then_inc(ln_chain, 1)
                dve.wait_ge(ln_chain, INIT + base + 2)
                V.scalar_tensor_tensor(ln_t[:], ln_v[:], -0.5, ln_y[:], ALU.mult, ALU.mult).then_inc(ln_chain, 1)
                dve.wait_ge(ln_chain, INIT + base + 3)
                V.tensor_tensor(ln_u[:], ln_t[:], ln_y[:], ALU.mult).then_inc(ln_chain, 1)
                dve.wait_ge(ln_chain, INIT + base + 4)
                V.scalar_tensor_tensor(ln_r[:], ln_u[:], 1.5, ln_y[:], ALU.add, ALU.mult).then_inc(ln_chain, 1)
                dve.wait_ge(ln_chain, INIT + base + 5)
                for g in range(RG):
                    V.tensor_scalar(xn[:, g, :], xres[:, g, :], ln_mv[:, g, 0:1], ln_r[:, g:g + 1],
                                    ALU.subtract, ALU.mult).then_inc(xn_ready, 1)
                dve.wait_ge(xn_ready, INIT + m * RG + RG)
                for g in range(RG):
                    last = V.tensor_tensor(xres[:, g, :], xres[:, g, :], bo[:, ds(m, 1), :].rearrange(
                        "p a d -> p (a d)"), ALU.add)
                    last.then_inc(ln_chain if g < 3 else xb_ready, 1)
                for c in range(DC):
                    dve.wait_ge(xt_mm, INIT + m * DC + c + 1)
                    at = m * (2 * DC) + (COL_LN + c)
                    V.tensor_scalar(ht32[:, c, :], LN_BANK[c][:, 0:ROWS], col[:, ds(at, 1)], col[:, ds(at + DC, 1)],
                                    ALU.mult, ALU.add).then_inc(h32_ready, 1)
                for c in range(DC):
                    dve.wait_ge(h_hi, INIT + m * DC + c + 1)
                    V.tensor_tensor(ht[:, LO, c, :], ht32[:, c, :], as_f32(ht[:, HI, c, :]),
                                    ALU.subtract).then_inc(h_lo, 1)

            def bank_max(k, n):
                dve.wait_ge(s_mm, INIT + n * 3 + k + 1)
                lo, hi = SPANS[k]
                V.tensor_reduce(mx[:, k:k + 1], logits[:, lo:hi], X, ALU.max).then_inc(mx_step, 1)

            def part_max(tile, n):
                dve.wait_ge(mx_step, INIT + n * 4 + 2)
                V.tensor_scalar(mx[:, 3:4], mx[:, 0:1], mx[:, 1:2], lb[:, ds(tile, 1)],
                                ALU.max, ALU.max).then_inc(mx_step, 1)

            def row_max(tile, n):
                dve.wait_ge(mx_step, INIT + n * 4 + 4)
                V.tensor_scalar(neg_max[:, ds(tile, 1)], mx[:, 2:3], mx[:, 3:4], -1.0,
                                ALU.max, ALU.mult).then_inc(max_ready, 1)

            def denominators(tile, n):
                at = ds(tile, 1)
                dve.wait_ge(exp_done, INIT + n + 1)
                dve.wait_ge(pe_done, INIT + n + 1)
                V.tensor_tensor(den[:, at], row_sum[:, at], p_extra[:, at], ALU.add).then_inc(den_ready, 1)
                dve.wait_ge(den_ready, INIT + n + 1)
                V.reciprocal(rden[:, at], den[:, at]).then_inc(rden_ready, 1)
                dve.wait_ge(rden_ready, INIT + n + 1)
                V.tensor_tensor(pn_extra[:, at], p_extra[:, at], rden[:, at], ALU.mult).then_inc(pn_ready, 1)

            def output_sum(m):
                dve.wait_ge(xb_ready, INIT + m + 1)
                for g in range(RG):
                    dve.wait_ge(ylo_ready, INIT + m * RG + g + 1)
                    V.tensor_tensor(xres[:, g, :], Y_BANK[g][0:RGP, 0:D], xres[:, g, :], ALU.add).then_inc(xs_ready, 1)
                    dve.wait_ge(xs_ready, INIT + m * RG + g + 1)
                    V.tensor_tensor(xres[:, g, :], xres[:, g, :], y_lo[g % 2][:], ALU.add).then_inc(x_ready, 1)

            start(dve, "dve")
            dve.wait_ge(consts_in, 16 * N_CONSTS)
            dve.wait_ge(setup_step, INIT + 3)
            V.tensor_reduce(cq[:], hprod[:], X, ALU.add).then_inc(cq_ready, 1)

            with dve.Fori(0, LAYERS) as l:
                norm(l)
                with dve.Fori(0, QUADS) as quad:
                    for pair in range(2):
                        n = l * 8 + quad * 2 + pair
                        for s in range(2):
                            h = pair * 2 + s
                            dve.wait_ge(q_hi[s], INIT + n + 1)
                            V.scalar_tensor_tensor(qh[s][:, LO, :], Q_BANK[s][:, 0:ROWS],
                                                   col[:, ds(l * H + quad * 4 + (COL_BQ + h), 1)],
                                                   as_f32(qh[s][:, HI, :]), ALU.add, ALU.subtract).then_inc(q_lo[s], 1)
                        for s in range(2):
                            dve.wait_ge(gp_ready[s], INIT + n + 1)
                            V.tensor_reduce(g_cols[:, :, ds(quad * 4 + (pair * 2 + s), 1)], g_prod[s][:],
                                            X, ALU.add).then_inc(gp_used[s], 1)
                        for s in range(2):
                            dve.wait_ge(w_used[s], INIT + l * 16 + quad * 2 + (pair + 1))
                            V.tensor_scalar(head_rows_of(quad * 4 + (pair * 2 + s))[:, 1],
                                            batch_qrows(QP_BANK[s][1][:, 0:ROWS]), SCALE, None,
                                            ALU.mult).then_inc(qp_out1[s], 1)
                dve.wait_ge(lb_mm, INIT + l + 1)
                dve.wait_ge(cq_ready, INIT + 1)
                V.tensor_scalar(lb_rows[:], batch_qrows(bank[7][0:H, 0:ROWS]), cq[:, ds(l, 1)], SCALE,
                                ALU.add, ALU.mult).then_inc(lb_rows_ready, 1)

                tiles = l * NT
                for k in range(2):
                    bank_max(k, tiles)
                dve.wait_ge(lb_tr, INIT + l + 1)
                V.tensor_copy(lb[:], bank[6][:, 0:NT]).then_inc(lb_ready, 1)
                dve.wait_ge(lb_ready, INIT + l + 1)
                part_max(0, tiles)
                bank_max(2, tiles)
                row_max(0, tiles)

                def row_tile(tile, has_next):
                    n = tiles + tile
                    for g in range(NG):
                        dve.wait_ge(pt_hi, INIT + n * NG + g + 1)
                        V.tensor_tensor(pt[:, LO, g, :], TP[g][0:CT, :], as_f32(pt[:, HI, g, :]),
                                        ALU.subtract).then_inc(pt_lo, 1)
                        if has_next:
                            bank_max(g, n + 1)
                            if g == 1:
                                part_max(tile + 1, n + 1)
                    if has_next:
                        row_max(tile + 1, n + 1)
                    denominators(tile, n)
                    dve.wait_ge(onlo_ready, INIT + n + 1)
                    dve.wait_ge(ot_mm, INIT + n)
                    V.scalar_tensor_tensor(on[:], O_BANK[:, 0:D], rden[:, ds(tile, 1)], on_lo[:],
                                           ALU.mult, ALU.add).then_inc(on_ready, 1)

                row_tile(0, True)
                with dve.Fori(0, B - 1) as b:
                    for r in range(1, TILES + 1):
                        row_tile(b * TILES + r, True)
                for r in range(1, TILES):
                    row_tile((B - 1) * TILES + r, r < TILES - 1)
                dve.wait_ge(pb_tr, INIT + l + 1)
                V.tensor_copy(pb_tiles[:], bank[7][0:NT, 0:P]).then_inc(pb_ready, 1)

                def split_lo(h, s, n):
                    dve.wait_ge(oth_hi[s], INIT + n + 1)
                    V.tensor_tensor(oth[s][:, LO].rearrange("p c (b q) -> p c b q", b=B), head_rows_of(h),
                                    as_f32(oth[s][:, HI]).rearrange("p c (b q) -> p c b q", b=B),
                                    ALU.subtract).then_inc(oth_lo[s], 1)

                def heads(quad_h, n, last_quad):
                    for u in range(4):
                        s, k = u % 2, u // 2
                        dve.wait_ge(c_hi[s], INIT + n + k + 1)
                        V.scalar_tensor_tensor(cs[s][:, LO, :], C_BANK[s][:, 0:ROWS],
                                               col[:, ds(l * H + quad_h + (COL_BV + u), 1)],
                                               as_f32(cs[s][:, HI, :]), ALU.add, ALU.subtract).then_inc(c_lo[s], 1)
                        if not (last_quad and k == 1):
                            split_lo(quad_h + (u + 2), s, n + k + 1)

                for s in range(2):
                    split_lo(s, s, l * 8)
                with dve.Fori(0, QUADS - 1) as quad:
                    heads(quad * 4, l * 8 + quad * 2, False)
                heads(4 * (QUADS - 1), l * 8 + 6, True)
                output_sum(l)

            norm(LAYERS)
            with dve.Fori(0, FT // 4) as quad:
                for pair in range(2):
                    n = quad * 2 + (16 + pair)
                    for s in range(2):
                        dve.wait_ge(c_hi[s], INIT + n + 1)
                        V.tensor_tensor(cs[s][:, LO, :], g32[s][:], as_f32(cs[s][:, HI, :]),
                                        ALU.subtract).then_inc(c_lo[s], 1)
            output_sum(LAYERS)


def kernel(**inputs):
    import numpy as np
    import concourse.bacc as bacc
    from concourse.bass_utils import run_bass_kernel_spmd as run

    a = {k.removeprefix("L0_xattn_"): np.asarray(v) for k, v in inputs.items()}

    def both(name):
        return np.stack([a[f"{name}1"], a[f"{name}2"]])

    def wide(wm):
        return wm.reshape(DC, P, -1, P).transpose(2, 1, 0, 3).reshape(-1, P, D)

    def pack(first, second):
        return np.concatenate([first, second], axis=2)

    tiles = []
    for n in "12":
        tiles.append(pack(wide(a["wq" + n]), a["wk" + n].reshape(D, H, K).transpose(1, 2, 0)))
        tiles.append(pack(wide(a["wv" + n]), a["wo" + n].reshape(H, K, D)))
    tiles.append(pack(wide(a["w_fc1"]), a["w_fc2"].reshape(FT, P, D)))

    norms = [a[n + part].reshape(DC, P) for n in ("ln1", "ln2", "ln_mlp") for part in ("_scale", "_offset")]
    cols = np.concatenate([*norms, both("bq").reshape(-1, P), both("bv").reshape(-1, P),
                           a["b_fc1"].reshape(FT, P)]).T
    bias_k, bias_v = both("bias_k").reshape(LAYERS, H, K), both("bias_v").reshape(LAYERS, H, K)
    bk, bv, bq = (both(n).reshape(LAYERS, H, K) for n in ("bk", "bv", "bq"))
    ctx_in = a["ctx_2048"]
    mask = np.zeros((EXTRA, H), np.float32)
    for g in range(3):
        mask[32 * g:32 * g + H] = np.eye(H, dtype=np.float32)

    arrays = {
        "x_rows": a["x"].reshape(RG, RGP, D).transpose(1, 0, 2),
        "ctx_nat": ctx_in.reshape(B, PIECES, PCT, CT, D).transpose(0, 1, 3, 2, 4),
        "ctx_tr": ctx_in.reshape(B, PIECES, PT_COLS, DC, P).transpose(0, 1, 4, 3, 2),
        "weights": np.concatenate(tiles),
        "cols": cols,
        "out_bias": np.stack([a["bo1"], a["bo2"], a["b_fc2"]]),
        "key_rows": np.stack([bias_k, bk], axis=1).reshape(LAYERS, 2, H * K),
        "head_rows": np.stack([bias_k, bk, bq]).transpose(2, 0, 1, 3),
        "value_rows": np.stack([bias_v, bv]).transpose(2, 0, 1, 3),
        "ident_in": np.eye(P, dtype=np.float32),
        "mask_in": mask,
    }
    arrays = {k: np.ascontiguousarray(v) for k, v in arrays.items()}
    nc = bacc.Bacc("TRN2", target_bir_lowering=False, num_devices=1)
    aps = {k: nc.dram_tensor(k, v.shape, F32, kind="ExternalInput").ap() for k, v in arrays.items()}
    for k in ("lb_scratch", "pb_scratch"):
        aps[k] = nc.dram_tensor(k, (B * FLAT,), F32, kind="Internal").ap()
    out = nc.dram_tensor("out_rows", (RGP, RG, D), F32, kind="ExternalOutput").ap()
    build(nc, **aps, out=out)
    got = run(nc, [arrays], core_ids=[0]).results[0]["out_rows"]
    return got.transpose(1, 0, 2).reshape(B, Q, D)
```

```python
import concourse.bass as bass
from concourse import mybir
from contextlib import ExitStack

F32 = mybir.dt.float32
F32R = mybir.dt.float32r
ALU = mybir.AluOpType
ACT = mybir.ActivationFunctionType
X = mybir.AxisListType.X
ds = bass.ds

LAYERS, B, Q, D, H, K, T, F = 2, 8, 56, 256, 16, 128, 1500, 1024
P = 128
DC = D // P
ROWS = B * Q
RG = 4
RGP = ROWS // RG
FLAT = Q * H
TILES = FLAT // P
TQ = P // H
NT = B * TILES
CT = 125
NCT = T // CT
GRP = 4
NG = NCT // GRP
PIECES = 4
PCT = NCT // PIECES
PT_COLS = T // PIECES
BANK = 512
SPANS = [(0, BANK), (BANK, 2 * BANK), (2 * BANK, T)]
FT = F // P
QUADS = H // 4
JOBS_Q, JOBS_L = H, 2 * H
SCALE = float(K) ** -0.5
LN_EPS = 1e-5
HI, LO = 0, 1
TERMS = ((HI, HI), (HI, LO), (LO, HI))

COL_LN = 0
COL_BQ = COL_LN + 3 * 2 * DC
COL_BV = COL_BQ + LAYERS * H
COL_B1 = COL_BV + LAYERS * H
N_COLS = COL_B1 + FT
INIT = 1
LN_CHAIN = 4
EXTRA = 80
SPREAD = (TQ - 1) * H


def build(nc, x_rows, ctx_nat, ctx_tr, weights, cols, out_bias, key_rows, head_rows, value_rows,
          ident_in, mask_in, pick_in, spread_in, out):
    stack = ExitStack()
    with stack:
        place_at = [(nc.sbuf_base + 63) // 64 * 64]

        def sb(name, shape, dtype):
            size = 4
            for n in shape[1:]:
                size *= n
            at = place_at[0]
            place_at[0] += (size + 31) // 32 * 32
            return nc.alloc_sbuf_tensor_at(name, shape, dtype, offset=at)

        def sem(name):
            return stack.enter_context(nc.semaphore(name))

        qt_at = place_at[0]
        qt = sb("qt", [P, DC, B, FLAT], F32)
        nat_stage = sb("nat_stage", [CT, PCT, D], F32)
        tr_stage = sb("tr_stage", [P, DC, PT_COLS], F32)
        xres = sb("xres", [RGP, RG, D], F32)
        w_raw = [sb(f"w_raw{s}", [P, 2 * D], F32) for s in range(2)]
        w = [sb(f"w{u}", [P, 2, 2 * D], F32R) for u in range(2)]
        ident = sb("ident", [P, P], F32)
        col = sb("col", [P, N_COLS], F32)
        bo = sb("bo", [RGP, 3, D], F32)
        lb = sb("lb", [P, NT], F32)
        neg_max = sb("neg_max", [P, NT], F32)
        row_sum = sb("row_sum", [P, NT], F32)
        p_extra = sb("p_extra", [P, NT], F32)
        den = sb("den", [P, NT], F32)
        rden = sb("rden", [P, NT], F32)
        pn_extra = sb("pn_extra", [P, NT], F32)
        mx = sb("mx", [P, 4], F32)
        g_cols = sb("g_cols", [P, DC, H], F32)
        cq = sb("cq", [H, LAYERS], F32)
        dv = sb("dv", [EXTRA, LAYERS, K], F32)
        mask = sb("mask", [EXTRA, H], F32)
        pick = sb("pick", [P, TQ, EXTRA], F32)
        spread = sb("spread", [H, SPREAD + P], F32)
        ln_stat = sb("ln_stat", [RGP, RG, 6], F32)
        ln_mv = sb("ln_mv", [RGP, RG, 2], F32)
        ln_v = sb("ln_v", [RGP, RG], F32)
        minus_half = sb("minus_half", [RGP, RG], F32)
        ln_y = sb("ln_y", [RGP, RG], F32)
        ln_t = sb("ln_t", [RGP, RG], F32)
        ln_u = sb("ln_u", [RGP, RG], F32)
        ln_r = sb("ln_r", [RGP, RG], F32)

        pt = sb("pt", [CT, 2, NG, GRP * P], F32R)
        at_attention = place_at[0]
        e = sb("e", [P, T + 4], F32)
        on = sb("on", [P, D], F32)
        on_lo = sb("on_lo", [P, D], F32)
        qs = sb("qs", [P, 2, DC, P], F32R)
        after_attention = place_at[0]
        place_at[0] = at_attention
        g_prod = [sb(f"g_prod{s}", [P, DC, K], F32) for s in range(2)]
        w += [sb(f"w{u}", [P, 2, 2 * D], F32R) for u in (2, 3)]
        place_at[0] = max(place_at[0], after_attention)

        N_TR, N_NAT = DC * 2 * T, NCT * 2 * D
        slot_words = N_TR + N_NAT
        ctx = sb("ctx", [P, 2, slot_words], F32R)
        end = place_at[0]
        assert end <= nc.sbuf_usable_end, (end, nc.sbuf_usable_end)

        scratch_at = end - slot_words * 4
        place_at[0] = scratch_at
        xn = sb("xn", [RGP, RG, D], F32)
        ht32 = sb("ht32", [P, DC, ROWS], F32)
        ht = sb("ht", [P, 2, DC, ROWS], F32R)
        after_ln = place_at[0]
        qh = [sb(f"qh{s}", [P, 2, ROWS], F32R) for s in range(2)]
        dk_all = sb("dk_all", [P, H * K], F32)
        lb_rows = sb("lb_rows", [H, ROWS], F32)
        key_row = sb("key_row", [1, 2, H * K], F32)
        assert place_at[0] <= end, (place_at[0], end)
        place_at[0] = after_ln
        cs = [sb(f"cs{s}", [P, 2, ROWS], F32R) for s in range(2)]
        pm = [sb(f"pm{s}", [EXTRA, ROWS], F32R) for s in range(2)]
        p80 = sb("p80", [EXTRA, ROWS], F32R)
        dv80 = sb("dv80", [EXTRA, K], F32R)
        oth_at = place_at[0]
        oth = [sb(f"oth{s}", [P, 2, DC, ROWS], F32R) for s in range(2)]
        assert place_at[0] <= end
        place_at[0] = oth_at
        g32 = [sb(f"g32_{s}", [P, ROWS], F32) for s in range(2)]
        assert place_at[0] <= end
        place_at[0] = qt_at
        hrow = sb("hrow", [H, 3, LAYERS, K], F32)
        vrow = sb("vrow", [EXTRA, 2, LAYERS, K], F32)
        hprod = sb("hprod", [H, LAYERS, K], F32)

        logits = stack.enter_context(nc.psum_tensor("logits", [P, 3 * BANK], F32))
        single = [stack.enter_context(nc.psum_tensor(f"bank{i}", [P, BANK], F32)) for i in range(3, 8)]
        bank = [logits[:, i * BANK:(i + 1) * BANK] for i in range(3)] + [t[:, :] for t in single]
        TP = [bank[3], bank[4], bank[7]]
        O_BANK, OT_BANK = bank[5], bank[6]
        LN_BANK = [bank[6], bank[7]]
        Q_BANK = [bank[3], bank[4]]
        QP_BANK = [[bank[5], bank[6]], [bank[0], bank[1]]]
        C_BANK = [bank[3], bank[4]]
        Y_BANK = [bank[0], bank[1], bank[2], bank[5]]

        zeroed = sem("zeroed")
        x_in = sem("x_in")
        consts_in = sem("consts_in")
        setup_step = sem("setup_step")
        cq_step, cq_ready, dv_ready = sem("cq_step"), sem("cq_ready"), sem("dv_ready")
        nat_in, tr_in = sem("nat_in"), sem("tr_in")
        ctx_hi, ctx_lo = sem("ctx_hi"), sem("ctx_lo")
        w_in = [sem(f"w_in{s}") for s in range(2)]
        w_hi = [sem(f"w_hi{u}") for u in range(4)]
        w_lo = [sem(f"w_lo{u}") for u in range(4)]
        w_used = [sem(f"w_used{u}") for u in range(4)]
        krow_in, dk_step = sem("krow_in"), sem("dk_step")
        gp_ready = [sem(f"gp_ready{s}") for s in range(2)]
        gp_used = [sem(f"gp_used{s}") for s in range(2)]
        ln_stats, ln_aggr, ln_chain, ln_pow = sem("ln_stats"), sem("ln_aggr"), sem("ln_chain"), sem("ln_pow")
        xn_ready, xt_mm = sem("xn_ready"), sem("xt_mm")
        h32_ready, h_hi, h_lo = sem("h32_ready"), sem("h_hi"), sem("h_lo")
        q_mm = [sem(f"q_mm{s}") for s in range(2)]
        q_hi = [sem(f"q_hi{s}") for s in range(2)]
        q_lo = [sem(f"q_lo{s}") for s in range(2)]
        qp_mm = [sem(f"qp_mm{s}") for s in range(2)]
        qp_out0 = [sem(f"qp_out0_{s}") for s in range(2)]
        qp_out1 = [sem(f"qp_out1_{s}") for s in range(2)]
        lb_mm, lb_rows_ready, lb_spread, lb_ready = (
            sem("lb_mm"), sem("lb_rows_ready"), sem("lb_spread"), sem("lb_ready"))
        qs_hi, qs_lo = sem("qs_hi"), sem("qs_lo")
        s_mm = sem("s_mm")
        mx_step, max_ready = sem("mx_step"), sem("max_ready")
        exp_done, pe_done = sem("exp_done"), sem("pe_done")
        den_ready, rden_ready, pn_ready = sem("den_ready"), sem("rden_ready"), sem("pn_ready")
        tp_mm, pt_hi, pt_lo = sem("tp_mm"), sem("pt_hi"), sem("pt_lo")
        pv_mm, onlo_ready, on_ready = sem("pv_mm"), sem("onlo_ready"), sem("on_ready")
        ot_mm, ot_out = sem("ot_mm"), sem("ot_out")
        pn_picked = sem("pn_picked")
        dv80_step, p80_hi, p80_lo = sem("dv80_step"), sem("p80_hi"), sem("p80_lo")
        pm_ready = [sem(f"pm_ready{s}") for s in range(2)]
        oth_hi = [sem(f"oth_hi{s}") for s in range(2)]
        oth_lo = [sem(f"oth_lo{s}") for s in range(2)]
        c_mm = [sem(f"c_mm{s}") for s in range(2)]
        c_hi = [sem(f"c_hi{s}") for s in range(2)]
        c_lo = [sem(f"c_lo{s}") for s in range(2)]
        g32_ready = [sem(f"g32_ready{s}") for s in range(2)]
        y_mm, xb_ready, x_ready = sem("y_mm"), sem("xb_ready"), sem("x_ready")
        out_written = sem("out_written")
        settled = sem("settled")

        N_CONSTS = 10

        def settle(eng):
            eng.sem_inc(settled, 1)

        started_by = {
            "pe": [*w_used, xt_mm, *q_mm, *qp_mm, lb_mm, lb_spread, s_mm, tp_mm, pv_mm, ot_mm, pn_picked, *c_mm,
                   y_mm],
            "act": [*w_hi, h_hi, *q_hi, *qp_out0, exp_done, pe_done, pt_hi, onlo_ready, ot_out, p80_hi, *oth_hi,
                    *c_hi, *g32_ready],
            "dve": [x_ready, ln_stats, ln_aggr, ln_chain, xn_ready, h32_ready, h_lo, cq_step, cq_ready, dv_ready, *gp_ready, *gp_used,
                    *q_lo, *qp_out1, lb_rows_ready, ctx_hi, lb_ready, mx_step, max_ready, den_ready, rden_ready,
                    pn_ready, pt_lo, on_ready, p80_lo, *oth_lo, *c_lo, xb_ready],
            "pool": [zeroed, setup_step, ctx_lo, *w_lo, ln_pow, dk_step, qs_hi, qs_lo, dv80_step, *pm_ready],
        }

        def start(eng, name):
            for counter in started_by[name]:
                eng.sem_inc(counter, INIT)

        qt_flat = qt[:].rearrange("p c b f -> p c (b f)")

        def head_rows_of(h):
            return qt[:].rearrange("p c b (q h) -> p c (b q) h", h=H)[:, :, :, ds(h, 1)].rearrange(
                "p c r a -> p c (r a)")

        def ctx_tr_part(slot, half, part, lo, hi):
            at = (half * 2 + part) * T
            return ctx[:, ds(slot, 1), at + lo:at + hi].rearrange("p a t -> p (a t)")

        def ctx_nat_tile(slot, t, width):
            at = N_TR + t * 2 * D
            return ctx[0:CT, ds(slot, 1), at:at + width].rearrange("p a t -> p (a t)")

        def as_f32(ap):
            return ap.bitcast(F32)

        def piece_views(slot, p):
            nat = ctx[0:CT, ds(slot, 1), ds(p * (PCT * 2 * D) + N_TR, PCT * 2 * D)].rearrange(
                "p a (t c d) -> p (a t) c d", t=PCT, c=2)
            tr = ctx[:, ds(slot, 1), 0:N_TR].rearrange("p a (c h t) -> p (a c) h t", c=DC, h=2)
            return nat, tr[:, :, :, ds(p * PT_COLS, PT_COLS)]

        block = stack.enter_context(nc.Block())

        @block.sync
        def _(sp):
            def load_weight(job, u, n):
                before = (u + 2) % 4
                sp.wait_ge(w_lo[before], INIT + n + u // 2)
                sp.dma_start(w_raw[u % 2][:], weights[ds(job, 1)].rearrange("a p n -> (a p) n")).then_inc(
                    w_in[u % 2], 16)

            def load_piece(batch, n, p):
                sp.wait_ge(ctx_lo, INIT + 2 * n)
                sp.dma_start(nat_stage[:], ctx_nat[ds(batch, 1), ds(p, 1)].rearrange(
                    "a b t c d -> (a b t) c d")).then_inc(nat_in, 16)
                sp.dma_start(tr_stage[:], ctx_tr[ds(batch, 1), ds(p, 1)].rearrange(
                    "a b p c t -> (a b p) c t")).then_inc(tr_in, 16)

            sp.dma_start(xres[:], x_rows).then_inc(x_in, 16)
            sp.dma_start(ident[:], ident_in).then_inc(consts_in, 16)
            sp.dma_start(col[:], cols).then_inc(consts_in, 16)
            sp.dma_start(hrow[:], head_rows).then_inc(consts_in, 16)
            sp.wait_ge(zeroed, INIT + 1)
            for g in range(3):
                sp.dma_start(vrow[32 * g:32 * g + H], value_rows).then_inc(consts_in, 16)
            sp.dma_start(bo[:], out_bias.partition_broadcast(RGP)).then_inc(consts_in, 16)
            sp.dma_start(mask[:], mask_in).then_inc(consts_in, 16)
            sp.dma_start(pick[:], pick_in).then_inc(consts_in, 16)
            sp.dma_start(spread[:], spread_in).then_inc(consts_in, 16)

            with sp.Fori(0, LAYERS) as l:
                sp.wait_ge(x_ready, INIT + l * RG)
                settle(sp)
                sp.dma_start(key_row[:], key_rows[ds(l, 1)]).then_inc(krow_in, 16)
                with sp.Fori(0, QUADS) as quad:
                    for u in range(4):
                        sp.wait_ge(gp_ready[u % 2], INIT + l * 8 + quad * 2 + u // 2)
                        settle(sp)
                        load_weight(l * JOBS_L + quad * 4 + u, u, l * 8 + quad)
                    load_piece(0, l * (B * PIECES) + quad, quad)

                with sp.Fori(0, B - 1) as b:
                    for p in range(PIECES):
                        load_piece(b + 1, l * (B * PIECES) + b * PIECES + PIECES + p, p)

                for s in range(2):
                    sp.wait_ge(gp_ready[s], INIT + l * 8 + 8)
                settle(sp)
                with sp.Fori(0, QUADS) as quad:
                    for u in range(4):
                        load_weight(l * JOBS_L + JOBS_Q + quad * 4 + u, u, l * 8 + quad + 4)

            with sp.Fori(0, FT // 4) as quad:
                for u in range(4):
                    load_weight(LAYERS * JOBS_L + quad * 4 + u, u, LAYERS * 8 + quad)

            sp.wait_ge(x_ready, INIT + 3 * RG)
            sp.dma_start(out, xres[:]).then_inc(out_written, 16)
            sp.wait_ge(out_written, 16)

        @block.gpsimd
        def _(pool):
            def weight_lo(u, n):
                pool.wait_ge(w_hi[u], INIT + n + 1)
                settle(pool)
                nc.gpsimd.tensor_tensor(w[u][:, LO, :], w_raw[u % 2][:], as_f32(w[u][:, HI, :]),
                                        ALU.subtract).then_inc(w_lo[u], 1)

            def piece_lo(slot, n, p):
                nat, tr = piece_views(slot, p)
                pool.wait_ge(ctx_hi, INIT + n * 2 + 1)
                settle(pool)
                nc.gpsimd.tensor_tensor(nat[:, :, LO, :], nat_stage[:], as_f32(nat[:, :, HI, :]),
                                        ALU.subtract).then_inc(ctx_lo, 1)
                pool.wait_ge(ctx_hi, INIT + n * 2 + 2)
                settle(pool)
                nc.gpsimd.tensor_tensor(tr[:, :, LO, :], tr_stage[:], as_f32(tr[:, :, HI, :]),
                                        ALU.subtract).then_inc(ctx_lo, 1)

            def split_q(tile, n):
                src = qt_flat[:, :, ds(tile * P, P)]
                nc.gpsimd.tensor_copy(qs[:, HI], src).then_inc(qs_hi, 1)
                pool.wait_ge(qs_hi, INIT + n + 1)
                settle(pool)
                nc.gpsimd.tensor_tensor(qs[:, LO], src, as_f32(qs[:, HI]), ALU.subtract).then_inc(qs_lo, 1)

            def norm(m):
                pool.wait_ge(ln_chain, INIT + m * LN_CHAIN + 1)
                settle(pool)
                nc.gpsimd.tensor_tensor(ln_y[:], ln_v[:], minus_half[:], ALU.pow).then_inc(ln_pow, 1)

            start(pool, "pool")
            nc.gpsimd.memset(vrow[:], 0.0).then_inc(zeroed, 1)
            nc.gpsimd.memset(minus_half[:], -0.5).then_inc(setup_step, 1)
            pool.wait_ge(setup_step, INIT + 1)
            settle(pool)

            with pool.Fori(0, LAYERS) as l:
                norm(l)
                pool.wait_ge(krow_in, l * 16 + 16)
                settle(pool)
                nc.gpsimd.tensor_tensor(key_row[:, 0], key_row[:, 0], key_row[:, 1],
                                        ALU.subtract).then_inc(dk_step, 1)
                pool.wait_ge(dk_step, INIT + l * 2 + 1)
                settle(pool)
                nc.gpsimd.partition_broadcast(dk_all[:], key_row[:, 0], channels=P).then_inc(dk_step, 1)
                with pool.Fori(0, QUADS) as quad:
                    for u in range(4):
                        weight_lo(u, l * 8 + quad)
                    piece_lo(0, l * (B * PIECES) + quad, quad)

                for s in range(2):
                    pool.wait_ge(qp_out0[s], INIT + l * 8 + 8)
                    pool.wait_ge(qp_out1[s], INIT + l * 8 + 8)
                    pool.wait_ge(gp_used[s], INIT + l * 8 + 8)
                settle(pool)
                split_q(0, l * NT)
                pool.wait_ge(s_mm, INIT + (l * NT + 1) * 3)
                settle(pool)
                split_q(1, l * NT + 1)

                def next_q(tile):
                    pool.wait_ge(s_mm, INIT + (l * NT + tile + 2) * 3)
                    settle(pool)
                    split_q(tile + 2, l * NT + tile + 2)

                next_q(0)
                with pool.Fori(0, B - 1) as b:
                    for r in range(1, TILES + 1):
                        next_q(b * TILES + r)
                        if r <= PIECES:
                            piece_lo((b + 1) & 1, l * (B * PIECES) + b * PIECES + PIECES + r - 1, r - 1)
                for tile in range(NT - TILES + 1, NT - 2):
                    next_q(tile)

                pool.wait_ge(pv_mm, INIT + (l + 1) * NT)
                settle(pool)
                pool.wait_ge(dv_ready, INIT + 1)
                dv_l = dv[:, ds(l, 1), :].rearrange("p a k -> p (a k)")
                nc.gpsimd.tensor_copy(dv80[:], dv_l).then_inc(dv80_step, 1)
                pool.wait_ge(dv80_step, INIT + l * 2 + 1)
                settle(pool)
                nc.gpsimd.tensor_tensor(dv80[32:64], dv_l[32:64], as_f32(dv80[32:64]),
                                        ALU.subtract).then_inc(dv80_step, 1)
                pool.wait_ge(dv80_step, INIT + l * 2 + 2)

                def mask_extra(h, s, n):
                    pool.wait_ge(c_mm[s], INIT + n)
                    settle(pool)
                    nc.gpsimd.tensor_tensor(pm[s][:], as_f32(p80[:]), mask[:, ds(h, 1)].to_broadcast([EXTRA, ROWS]),
                                            ALU.mult).then_inc(pm_ready[s], 1)

                for u in range(2):
                    weight_lo(u, l * 8 + 4)
                pool.wait_ge(p80_lo, INIT + l + 1)
                for s in range(2):
                    mask_extra(s, s, l * 8)
                with pool.Fori(0, QUADS - 1) as quad:
                    for v in range(4):
                        u = (v + 2) % 4
                        weight_lo(u, l * 8 + quad + 4 + (v + 2) // 4)
                        mask_extra(quad * 4 + v + 2, v % 2, l * 8 + quad * 2 + v // 2 + 1)
                for s in range(2):
                    weight_lo(s + 2, l * 8 + 7)
                    mask_extra(H - 2 + s, s, l * 8 + 7)

            norm(LAYERS)
            with pool.Fori(0, FT // 4) as quad:
                for u in range(4):
                    weight_lo(u, LAYERS * 8 + quad)

        @block.tensor
        def _(pe):
            mm = nc.tensor.matmul

            def norm_transposes(m):
                pe.wait_ge(xn_ready, INIT + m * RG + RG)
                settle(pe)
                for c in range(DC):
                    for g in range(RG):
                        last = nc.tensor.transpose(LN_BANK[c][:, g * RGP:(g + 1) * RGP],
                                                   xn[:, g, c * P:(c + 1) * P], ident[0:RGP, 0:RGP])
                    last.then_inc(xt_mm, 1)

            def project(out_bank, u, moving, more):
                for c in range(DC):
                    for a, m in TERMS:
                        last = mm(out_bank, w[u][:, a, c * P:(c + 1) * P], moving(m, c),
                                  start=(c == 0 and (a, m) == (HI, HI)),
                                  stop=(not more and c == DC - 1 and (a, m) == (LO, HI)))
                return last

            def queries(u, n, job):
                s = u % 2
                pe.wait_ge(w_lo[u], INIT + job + 1)
                pe.wait_ge(q_lo[s], INIT + n)
                project(Q_BANK[s][:, 0:ROWS], u, lambda m, c: ht[:, m, c, :], False).then_inc(q_mm[s], 1)

            def carried_queries(u, n):
                s = u % 2
                pe.wait_ge(q_lo[s], INIT + n + 1)
                pe.wait_ge(qp_out0[s], INIT + n)
                pe.wait_ge(qp_out1[s], INIT + n)
                for c in range(DC):
                    for a, m in TERMS:
                        last = mm(QP_BANK[s][c][:, 0:ROWS], w[u][:, a, D + c * P:D + (c + 1) * P], qh[s][:, m, :],
                                  start=(a, m) == (HI, HI), stop=(a, m) == (LO, HI))
                    last.then_inc(qp_mm[s] if c == 0 else w_used[u], 1)

            def exp_transposes(g, n):
                for j in range(GRP):
                    t = g * GRP + j
                    last = nc.tensor.transpose(TP[g][0:CT, j * P:(j + 1) * P], e[:, t * CT:(t + 1) * CT], ident[:])
                last.then_inc(tp_mm, 1)

            def logit_bank(k, slot):
                lo, hi = SPANS[k]
                terms = [(c, a, m) for c in range(DC) for a, m in TERMS]
                for c, a, m in terms:
                    last = mm(logits[:, lo:hi], qs[:, a, c, :], ctx_tr_part(slot, c, m, lo, hi),
                              start=(c, a, m) == terms[0], stop=(c, a, m) == terms[-1])
                last.then_inc(s_mm, 1)

            def weighted_context(slot, n):
                pe.wait_ge(on_ready, INIT + n)
                for g in range(NG):
                    pe.wait_ge(pt_lo, INIT + n * NG + g + 1)
                    for j in range(GRP):
                        t = g * GRP + j
                        mm(O_BANK[:, 0:2 * D], pt[:, HI, g, j * P:(j + 1) * P], ctx_nat_tile(slot, t, 2 * D),
                           start=(t == 0), stop=(t == NCT - 1), skip_group_check=True)
                        last = mm(O_BANK[:, 0:D], pt[:, LO, g, j * P:(j + 1) * P], ctx_nat_tile(slot, t, D),
                                  start=False, stop=(t == NCT - 1), skip_group_check=True)
                last.then_inc(pv_mm, 1)

            def context_transposes(n):
                pe.wait_ge(on_ready, INIT + n + 1)
                pe.wait_ge(ot_out, INIT + n)
                for c in range(DC):
                    last = nc.tensor.transpose(OT_BANK[:, c * P:(c + 1) * P], on[:, c * P:(c + 1) * P], ident[:])
                last.then_inc(ot_mm, 1)

            def head_context(u, n, job, extra):
                s = u % 2
                pe.wait_ge(w_lo[u], INIT + job + 1)
                pe.wait_ge(c_lo[s], INIT + n)
                if extra:
                    pe.wait_ge(oth_lo[s], INIT + n + 1)
                    project(C_BANK[s][:, 0:ROWS], u, lambda m, c: oth[s][:, m, c, :], True)
                    pe.wait_ge(pm_ready[s], INIT + n + 1)
                    mm(C_BANK[s][:, 0:ROWS], dv80[:], pm[s][:], start=False, stop=True).then_inc(c_mm[s], 1)
                else:
                    project(C_BANK[s][:, 0:ROWS], u, lambda m, c: ht[:, m, c, :], False).then_inc(c_mm[s], 1)

            def output_rows(u, n, first, last_head):
                s = u % 2
                pe.wait_ge(c_lo[s], INIT + n + 1)
                for g in range(RG):
                    rows = slice(g * RGP, (g + 1) * RGP)
                    for a, m in TERMS:
                        last = mm(Y_BANK[g][0:RGP, 0:D], cs[s][:, a, rows], w[u][:, m, D:2 * D],
                                  start=first and (a, m) == (HI, HI), stop=last_head and (a, m) == (LO, HI))
                    if last_head and g < RG - 1:
                        last.then_inc(y_mm, 1)
                last.then_inc(w_used[u], 1)

            def output_quad(n, job, extra, first, last_quad):
                for pair in range(2):
                    for s in range(2):
                        head_context(pair * 2 + s, n + pair, job, extra)
                    for s in range(2):
                        output_rows(pair * 2 + s, n + pair, first and pair == 0 and s == 0,
                                    last_quad and pair == 1 and s == 1)

            start(pe, "pe")
            pe.wait_ge(consts_in, 16 * N_CONSTS)
            with pe.Fori(0, LAYERS) as l:
                norm_transposes(l)
                pe.wait_ge(h_lo, INIT + l * DC + DC)
                settle(pe)
                with pe.Fori(0, QUADS) as quad:
                    for pair in range(2):
                        for s in range(2):
                            queries(pair * 2 + s, l * 8 + quad * 2 + pair, l * 8 + quad)
                        for s in range(2):
                            carried_queries(pair * 2 + s, l * 8 + quad * 2 + pair)
                for s in range(2):
                    pe.wait_ge(gp_used[s], INIT + l * 8 + 8)
                for c in range(DC):
                    last = mm(bank[7][0:H, 0:ROWS], g_cols[:, c, :], ht32[:, c, :], start=(c == 0), stop=(c == DC - 1))
                last.then_inc(lb_mm, 1)

                tiles = l * NT
                pe.wait_ge(qs_lo, INIT + tiles + 1)
                pe.wait_ge(ctx_lo, INIT + l * (2 * B * PIECES) + 2 * PIECES)
                for k in range(3):
                    logit_bank(k, 0)
                pe.wait_ge(lb_rows_ready, INIT + l + 1)
                settle(pe)
                by_query = lb_rows[:].rearrange("h (t e) -> h t e", e=TQ)
                for j in range(TQ):
                    at = SPREAD - j * H
                    last = mm(bank[6][:, 0:NT], spread[:, at:at + P], by_query[:, :, j],
                              start=(j == 0), stop=(j == TQ - 1))
                last.then_inc(lb_spread, 1)

                def row_tile(tile, slot, next_slot, new_batch, has_next, has_before):
                    n = tiles + tile
                    pe.wait_ge(exp_done, INIT + n + 1)
                    pe.wait_ge(pt_lo, INIT + n * NG)
                    if has_next:
                        pe.wait_ge(qs_lo, INIT + n + 2)
                    if new_batch is not None:
                        pe.wait_ge(ctx_lo, INIT + l * (2 * B * PIECES) + new_batch * (2 * PIECES) + 2 * PIECES)
                    for k in range(NG):
                        exp_transposes(k, n)
                        if has_next:
                            logit_bank(k, next_slot)
                        if has_before and k == 0:
                            context_transposes(n - 1)
                    weighted_context(slot, n)

                row_tile(0, 0, 0, None, True, False)
                with pe.Fori(0, B - 1) as b:
                    for r in range(1, TILES + 1):
                        row_tile(b * TILES + r, (b + r // TILES) & 1, (b + (r + 1) // TILES) & 1,
                                 b + 1 if r == TILES - 1 else None, True, True)
                for r in range(1, TILES):
                    row_tile((B - 1) * TILES + r, (B - 1) & 1, (B - 1) & 1, None, r < TILES - 1, True)
                context_transposes(tiles + NT - 1)
                pe.wait_ge(pn_ready, INIT + tiles + NT)
                settle(pe)
                for j in range(TQ):
                    last = mm(bank[7][0:EXTRA, j * NT:(j + 1) * NT], pick[:, j, :], pn_extra[:],
                              start=(j == 0), stop=True, skip_group_check=True)
                last.then_inc(pn_picked, 1)

                output_quad(l * 8, l * 8 + 4, True, True, False)
                with pe.Fori(1, QUADS - 1) as quad:
                    output_quad(l * 8 + quad * 2, l * 8 + quad + 4, True, False, False)
                output_quad(l * 8 + 6, l * 8 + 7, True, False, True)

            norm_transposes(LAYERS)
            pe.wait_ge(h_lo, INIT + LAYERS * DC + DC)
            output_quad(LAYERS * 8, LAYERS * 8, False, True, False)
            output_quad(LAYERS * 8 + 2, LAYERS * 8 + 1, False, False, True)

        @block.scalar
        def _(act):
            go = nc.scalar.activation

            def weight_hi(u, n, n_raw):
                act.wait_ge(w_in[u % 2], n_raw * 16 + 16)
                act.wait_ge(w_used[u], INIT + n)
                go(w[u][:, HI, :], w_raw[u % 2][:], ACT.Copy).then_inc(w_hi[u], 1)

            def norm(m):
                for c in range(DC):
                    act.wait_ge(h32_ready, INIT + m * DC + c + 1)
                    go(ht[:, HI, c, :], ht32[:, c, :], ACT.Copy).then_inc(h_hi, 1)

            def exponentials(tile, n):
                at = ds(tile, 1)
                act.wait_ge(max_ready, INIT + n + 1)
                go(e[:, 0:T], logits[:, 0:T], ACT.Exp, bias=neg_max[:, at],
                   accum_out=row_sum[:, at]).then_inc(exp_done, 1)
                go(p_extra[:, at], lb[:, at], ACT.Exp, bias=neg_max[:, at]).then_inc(pe_done, 1)

            def transposed_context(tile, n):
                act.wait_ge(ot_mm, INIT + n + 1)
                go(qt_flat[:, :, ds(tile * P, P)], OT_BANK[:, 0:D].rearrange("p (c r) -> p c r", c=DC),
                   ACT.Copy).then_inc(ot_out, 1)

            start(act, "act")
            act.wait_ge(consts_in, 16 * N_CONSTS)
            with act.Fori(0, LAYERS) as l:
                for u in range(2):
                    weight_hi(u, l * 8, l * 16)
                norm(l)

                def query_quad(quad, last_quad):
                    for pair in range(2):
                        n = l * 8 + quad * 2 + pair
                        more = not (last_quad and pair == 1)
                        for s in range(2):
                            if more:
                                weight_hi((pair * 2 + s + 2) % 4, l * 8 + quad + pair, l * 16 + quad * 2 + pair + 1)
                            act.wait_ge(q_mm[s], INIT + n + 1)
                            if pair == 0:
                                act.wait_ge(w_used[s + 2], INIT + l * 8 + quad)
                            else:
                                act.wait_ge(w_used[s], INIT + l * 8 + quad + 1)
                            go(qh[s][:, HI, :], Q_BANK[s][:, 0:ROWS], ACT.Identity,
                               bias=col[:, ds(l * H + quad * 4 + (COL_BQ + pair * 2 + s), 1)]).then_inc(q_hi[s], 1)
                        for s in range(2):
                            act.wait_ge(qp_mm[s], INIT + n + 1)
                            go(head_rows_of(quad * 4 + (pair * 2 + s))[:, 0], QP_BANK[s][0][:, 0:ROWS],
                               ACT.Copy, scale=SCALE).then_inc(qp_out0[s], 1)

                with act.Fori(0, QUADS - 1) as quad:
                    query_quad(quad, False)
                query_quad(QUADS - 1, True)

                tiles = l * NT
                act.wait_ge(lb_ready, INIT + l + 1)
                exponentials(0, tiles)

                def row_tile(tile, has_next, has_before):
                    n = tiles + tile
                    for g in range(NG):
                        act.wait_ge(tp_mm, INIT + n * NG + g + 1)
                        go(pt[:, HI, g, :], TP[g][0:CT, :], ACT.Copy).then_inc(pt_hi, 1)
                        if g == 1 and has_before:
                            transposed_context(tile - 1, n - 1)
                    if has_next:
                        exponentials(tile + 1, n + 1)
                    act.wait_ge(pv_mm, INIT + n + 1)
                    act.wait_ge(rden_ready, INIT + n + 1)
                    act.wait_ge(on_ready, INIT + n)
                    go(on_lo[:], O_BANK[:, D:2 * D], ACT.Copy, scale=rden[:, ds(tile, 1)]).then_inc(onlo_ready, 1)

                row_tile(0, True, False)
                with act.Fori(0, B - 1) as b:
                    for r in range(1, TILES + 1):
                        row_tile(b * TILES + r, True, True)
                for r in range(1, TILES):
                    row_tile((B - 1) * TILES + r, r < TILES - 1, True)
                for u in range(2):
                    weight_hi(u, l * 8 + 4, l * 16 + 8)
                transposed_context(NT - 1, tiles + NT - 1)
                act.wait_ge(pn_picked, INIT + l + 1)
                go(p80[:].rearrange("p (t e) -> p t e", e=TQ), bank[7][0:EXTRA, 0:ROWS].rearrange(
                    "p (e t) -> p t e", e=TQ), ACT.Copy).then_inc(p80_hi, 1)
                act.wait_ge(ot_out, INIT + tiles + NT)

                def context_hi(h, s, n):
                    act.wait_ge(c_mm[s], INIT + n)
                    go(oth[s][:, HI], head_rows_of(h), ACT.Copy).then_inc(oth_hi[s], 1)

                def heads(quad, last_quad):
                    for v in range(4):
                        s, k = v % 2, v // 2
                        n = l * 8 + quad * 2 + k
                        act.wait_ge(c_mm[s], INIT + n + 1)
                        if k == 0:
                            act.wait_ge(w_used[s + 2], INIT + l * 8 + quad + 4)
                        else:
                            act.wait_ge(w_used[s], INIT + l * 8 + quad + 5)
                        go(cs[s][:, HI, :], C_BANK[s][:, 0:ROWS], ACT.Identity,
                           bias=col[:, ds(l * H + quad * 4 + (COL_BV + v), 1)]).then_inc(c_hi[s], 1)
                        if not (last_quad and k == 1):
                            context_hi(quad * 4 + (v + 2), s, n + 1)
                            weight_hi((v + 2) % 4, l * 8 + quad + 4 + k, l * 16 + quad * 2 + 9 + k)

                for s in range(2):
                    context_hi(s, s, l * 8)
                with act.Fori(0, QUADS - 1) as quad:
                    heads(quad, False)
                heads(QUADS - 1, True)

            for u in range(2):
                weight_hi(u, LAYERS * 8, LAYERS * 16)
            norm(LAYERS)
            for quad in range(FT // 4):
                for pair in range(2):
                    n = 16 + quad * 2 + pair
                    for s in range(2):
                        if not (quad == FT // 4 - 1 and pair == 1):
                            weight_hi((pair * 2 + s + 2) % 4, LAYERS * 8 + quad + pair,
                                      LAYERS * 16 + quad * 2 + pair + 1)
                        act.wait_ge(c_mm[s], INIT + n + 1)
                        act.wait_ge(c_lo[s], INIT + n)
                        go(g32[s][:], C_BANK[s][:, 0:ROWS], ACT.Gelu,
                           bias=col[:, ds(quad * 4 + (COL_B1 + pair * 2 + s), 1)]).then_inc(g32_ready[s], 1)
                    for s in range(2):
                        act.wait_ge(g32_ready[s], INIT + quad * 2 + (pair + 1))
                        act.wait_ge(w_used[(pair * 2 + s + 2) % 4], INIT + LAYERS * 8 + quad + pair)
                        go(cs[s][:, HI, :], g32[s][:], ACT.Copy).then_inc(c_hi[s], 1)

        @block.vector
        def _(dve):
            V = nc.vector

            def norm(m):
                base = m * LN_CHAIN
                for g in range(RG):
                    dve.wait_ge(x_ready, INIT + m * RG)
                    V.bn_stats(ln_stat[:, g, :], xres[:, g, :]).then_inc(ln_stats, 1)
                for g in range(RG):
                    dve.wait_ge(ln_stats, INIT + m * RG + g + 1)
                    settle(dve)
                    V.bn_aggr(ln_mv[:, g, :], ln_stat[:, g, :]).then_inc(ln_aggr, 1)
                dve.wait_ge(ln_aggr, INIT + m * RG + RG)
                V.tensor_scalar(ln_v[:], ln_mv[:, :, 1], LN_EPS, None, ALU.add).then_inc(ln_chain, 1)
                dve.wait_ge(ln_pow, INIT + m + 1)
                V.scalar_tensor_tensor(ln_t[:], ln_v[:], -0.5, ln_y[:], ALU.mult, ALU.mult).then_inc(ln_chain, 1)
                dve.wait_ge(ln_chain, INIT + base + 2)
                V.tensor_tensor(ln_u[:], ln_t[:], ln_y[:], ALU.mult).then_inc(ln_chain, 1)
                dve.wait_ge(ln_chain, INIT + base + 3)
                V.scalar_tensor_tensor(ln_r[:], ln_u[:], 1.5, ln_y[:], ALU.add, ALU.mult).then_inc(ln_chain, 1)
                dve.wait_ge(ln_chain, INIT + base + 4)
                for g in range(RG):
                    V.tensor_scalar(xn[:, g, :], xres[:, g, :], ln_mv[:, g, 0:1], ln_r[:, g:g + 1],
                                    ALU.subtract, ALU.mult).then_inc(xn_ready, 1)
                for c in range(DC):
                    dve.wait_ge(xt_mm, INIT + m * DC + c + 1)
                    at = m * (2 * DC) + (COL_LN + c)
                    V.tensor_scalar(ht32[:, c, :], LN_BANK[c][:, 0:ROWS], col[:, ds(at, 1)], col[:, ds(at + DC, 1)],
                                    ALU.mult, ALU.add).then_inc(h32_ready, 1)
                for c in range(DC):
                    dve.wait_ge(h_hi, INIT + m * DC + c + 1)
                    V.tensor_tensor(ht[:, LO, c, :], ht32[:, c, :], as_f32(ht[:, HI, c, :]),
                                    ALU.subtract).then_inc(h_lo, 1)
                for g in range(RG):
                    V.tensor_tensor(xres[:, g, :], xres[:, g, :], bo[:, ds(m, 1), :].rearrange(
                        "p a d -> p (a d)"), ALU.add).then_inc(xb_ready, 1)

            def piece_hi(slot, n, p):
                nat, tr = piece_views(slot, p)
                dve.wait_ge(nat_in, n * 16 + 16)
                V.tensor_copy(nat[:, :, HI, :], nat_stage[:]).then_inc(ctx_hi, 1)
                dve.wait_ge(tr_in, n * 16 + 16)
                V.tensor_copy(tr[:, :, HI, :], tr_stage[:]).then_inc(ctx_hi, 1)

            def bank_max(k, n):
                dve.wait_ge(s_mm, INIT + n * 3 + k + 1)
                lo, hi = SPANS[k]
                V.tensor_reduce(mx[:, k:k + 1], logits[:, lo:hi], X, ALU.max).then_inc(mx_step, 1)

            def part_max(tile, n):
                dve.wait_ge(mx_step, INIT + n * 4 + 2)
                V.tensor_scalar(mx[:, 3:4], mx[:, 0:1], mx[:, 1:2], lb[:, ds(tile, 1)],
                                ALU.max, ALU.max).then_inc(mx_step, 1)

            def row_max(tile, n):
                dve.wait_ge(mx_step, INIT + n * 4 + 4)
                V.tensor_scalar(neg_max[:, ds(tile, 1)], mx[:, 2:3], mx[:, 3:4], -1.0,
                                ALU.max, ALU.mult).then_inc(max_ready, 1)

            def denominators(tile, n):
                at = ds(tile, 1)
                dve.wait_ge(exp_done, INIT + n + 1)
                dve.wait_ge(pe_done, INIT + n + 1)
                V.tensor_tensor(den[:, at], row_sum[:, at], p_extra[:, at], ALU.add).then_inc(den_ready, 1)
                dve.wait_ge(den_ready, INIT + n + 1)
                V.reciprocal(rden[:, at], den[:, at]).then_inc(rden_ready, 1)
                dve.wait_ge(rden_ready, INIT + n + 1)
                V.tensor_tensor(pn_extra[:, at], p_extra[:, at], rden[:, at], ALU.mult).then_inc(pn_ready, 1)

            def output_sum(m, last_slot_jobs):
                dve.wait_ge(xb_ready, INIT + m * RG + RG)
                for g in range(RG):
                    if g < RG - 1:
                        dve.wait_ge(y_mm, INIT + m * (RG - 1) + g + 1)
                    else:
                        dve.wait_ge(w_used[3], INIT + last_slot_jobs)
                    V.tensor_tensor(xres[:, g, :], Y_BANK[g][0:RGP, 0:D], xres[:, g, :], ALU.add).then_inc(x_ready, 1)

            start(dve, "dve")
            dve.wait_ge(consts_in, 16 * N_CONSTS)
            V.tensor_tensor(hprod[:], hrow[:, 0], hrow[:, 1], ALU.subtract).then_inc(cq_step, 1)
            V.tensor_tensor(dv[:], vrow[:, 0], vrow[:, 1], ALU.subtract).then_inc(dv_ready, 1)
            dve.wait_ge(cq_step, INIT + 1)
            V.tensor_tensor(hprod[:], hprod[:], hrow[:, 2], ALU.mult).then_inc(cq_step, 1)
            dve.wait_ge(cq_step, INIT + 2)
            V.tensor_reduce(cq[:], hprod[:], X, ALU.add).then_inc(cq_ready, 1)
            dve.wait_ge(x_in, 16)

            with dve.Fori(0, LAYERS) as l:
                norm(l)
                dve.wait_ge(dk_step, INIT + l * 2 + 2)
                settle(dve)

                def key_bias_product(h, s, n):
                    dve.wait_ge(w_in[s], n * 16 + l * 128 + 16)
                    V.tensor_tensor(g_prod[s][:], w_raw[s][:, 0:DC * K].rearrange("p (c k) -> p c k", c=DC),
                                    dk_all[:, ds(h * K, K)].rearrange("p (a k) -> p a k", a=1).to_broadcast(
                                        [P, DC, K]), ALU.mult).then_inc(gp_ready[s], 1)
                    dve.wait_ge(gp_ready[s], INIT + n + 1)
                    V.tensor_reduce(g_cols[:, :, ds(h, 1)], g_prod[s][:], X, ALU.add).then_inc(gp_used[s], 1)

                def query_quad(quad, last_quad):
                    for pair in range(2):
                        n = l * 8 + quad * 2 + pair
                        for s in range(2):
                            h = pair * 2 + s
                            dve.wait_ge(q_hi[s], INIT + n + 1)
                            V.scalar_tensor_tensor(qh[s][:, LO, :], Q_BANK[s][:, 0:ROWS],
                                                   col[:, ds(l * H + quad * 4 + (COL_BQ + h), 1)],
                                                   as_f32(qh[s][:, HI, :]), ALU.add, ALU.subtract).then_inc(q_lo[s], 1)
                        if not (last_quad and pair == 1):
                            for s in range(2):
                                key_bias_product(quad * 4 + (pair * 2 + s + 2), s, n + 1)
                        for s in range(2):
                            dve.wait_ge(w_used[pair * 2 + s], INIT + l * 8 + quad + 1)
                            V.tensor_scalar(head_rows_of(quad * 4 + (pair * 2 + s))[:, 1],
                                            QP_BANK[s][1][:, 0:ROWS], SCALE, None, ALU.mult).then_inc(qp_out1[s], 1)
                    piece_hi(0, l * (B * PIECES) + quad, quad)

                for s in range(2):
                    key_bias_product(s, s, l * 8)
                with dve.Fori(0, QUADS - 1) as quad:
                    query_quad(quad, False)
                query_quad(QUADS - 1, True)
                dve.wait_ge(lb_mm, INIT + l + 1)
                dve.wait_ge(cq_ready, INIT + 1)
                V.tensor_scalar(lb_rows[:], bank[7][0:H, 0:ROWS], cq[:, ds(l, 1)], SCALE,
                                ALU.add, ALU.mult).then_inc(lb_rows_ready, 1)

                tiles = l * NT
                for k in range(2):
                    bank_max(k, tiles)
                dve.wait_ge(lb_spread, INIT + l + 1)
                V.tensor_copy(lb[:], bank[6][:, 0:NT]).then_inc(lb_ready, 1)
                dve.wait_ge(lb_ready, INIT + l + 1)
                part_max(0, tiles)
                bank_max(2, tiles)
                row_max(0, tiles)

                def row_tile(tile, has_next, piece=None):
                    n = tiles + tile
                    for g in range(NG):
                        dve.wait_ge(pt_hi, INIT + n * NG + g + 1)
                        V.tensor_tensor(pt[:, LO, g, :], TP[g][0:CT, :], as_f32(pt[:, HI, g, :]),
                                        ALU.subtract).then_inc(pt_lo, 1)
                        if has_next:
                            bank_max(g, n + 1)
                            if g == 1:
                                part_max(tile + 1, n + 1)
                    if has_next:
                        row_max(tile + 1, n + 1)
                    denominators(tile, n)
                    if piece is not None:
                        piece_hi(*piece)
                    dve.wait_ge(onlo_ready, INIT + n + 1)
                    dve.wait_ge(ot_mm, INIT + n)
                    V.scalar_tensor_tensor(on[:], O_BANK[:, 0:D], rden[:, ds(tile, 1)], on_lo[:],
                                           ALU.mult, ALU.add).then_inc(on_ready, 1)

                row_tile(0, True)
                with dve.Fori(0, B - 1) as b:
                    for r in range(1, TILES + 1):
                        piece = r <= PIECES
                        row_tile(b * TILES + r, True, (
                            (b + 1) & 1, l * (B * PIECES) + b * PIECES + PIECES + r - 1, r - 1) if piece else None)
                for r in range(1, TILES):
                    row_tile((B - 1) * TILES + r, r < TILES - 1)
                dve.wait_ge(p80_hi, INIT + l + 1)
                p80_l = p80[64:EXTRA].rearrange("p (t e) -> p t e", e=TQ)
                V.tensor_tensor(p80_l, bank[7][64:EXTRA, 0:ROWS].rearrange("p (e t) -> p t e", e=TQ),
                                as_f32(p80_l), ALU.subtract).then_inc(p80_lo, 1)

                def context_lo(h, s, n):
                    dve.wait_ge(oth_hi[s], INIT + n + 1)
                    V.tensor_tensor(oth[s][:, LO], head_rows_of(h), as_f32(oth[s][:, HI]),
                                    ALU.subtract).then_inc(oth_lo[s], 1)

                def heads(quad_h, n, last_quad):
                    for u in range(4):
                        s, k = u % 2, u // 2
                        dve.wait_ge(c_hi[s], INIT + n + k + 1)
                        V.scalar_tensor_tensor(cs[s][:, LO, :], C_BANK[s][:, 0:ROWS],
                                               col[:, ds(l * H + quad_h + (COL_BV + u), 1)],
                                               as_f32(cs[s][:, HI, :]), ALU.add, ALU.subtract).then_inc(c_lo[s], 1)
                        if not (last_quad and k == 1):
                            context_lo(quad_h + (u + 2), s, n + k + 1)

                for s in range(2):
                    context_lo(s, s, l * 8)
                with dve.Fori(0, QUADS - 1) as quad:
                    heads(quad * 4, l * 8 + quad * 2, False)
                heads(4 * (QUADS - 1), l * 8 + 6, True)
                output_sum(l, l * 8 + 8)

            norm(LAYERS)
            with dve.Fori(0, FT // 4) as quad:
                for pair in range(2):
                    n = quad * 2 + (16 + pair)
                    for s in range(2):
                        dve.wait_ge(c_hi[s], INIT + n + 1)
                        V.tensor_tensor(cs[s][:, LO, :], g32[s][:], as_f32(cs[s][:, HI, :]),
                                        ALU.subtract).then_inc(c_lo[s], 1)
            output_sum(LAYERS, LAYERS * 8 + FT // 4)


def kernel(**inputs):
    import numpy as np
    import concourse.bacc as bacc
    from concourse.bass_utils import run_bass_kernel_spmd as run

    a = {k.removeprefix("L0_xattn_"): np.asarray(v) for k, v in inputs.items()}

    def both(name):
        return np.stack([a[f"{name}1"], a[f"{name}2"]])

    def wide(wm):
        return wm.reshape(DC, P, -1, P).transpose(2, 1, 0, 3).reshape(-1, P, D)

    def pack(first, second):
        return np.concatenate([first, second], axis=2)

    tiles = []
    for n in "12":
        tiles.append(pack(wide(a["wq" + n]), a["wk" + n].reshape(D, H, K).transpose(1, 2, 0)))
        tiles.append(pack(wide(a["wv" + n]), a["wo" + n].reshape(H, K, D)))
    tiles.append(pack(wide(a["w_fc1"]), a["w_fc2"].reshape(FT, P, D)))

    norms = [a[n + part].reshape(DC, P) for n in ("ln1", "ln2", "ln_mlp") for part in ("_scale", "_offset")]
    cols = np.concatenate([*norms, both("bq").reshape(-1, P), both("bv").reshape(-1, P),
                           a["b_fc1"].reshape(FT, P)]).T
    bias_k, bias_v = both("bias_k").reshape(LAYERS, H, K), both("bias_v").reshape(LAYERS, H, K)
    bk, bv, bq = (both(n).reshape(LAYERS, H, K) for n in ("bk", "bv", "bq"))
    ctx_in = a["ctx_2048"]
    mask = np.zeros((EXTRA, H), np.float32)
    for g in range(3):
        mask[32 * g:32 * g + H] = np.eye(H, dtype=np.float32)

    pick = np.zeros((P, TQ, EXTRA), np.float32)
    for j in range(TQ):
        for g in range(3):
            pick[j * H:(j + 1) * H, j, 32 * g:32 * g + H] = np.eye(H, dtype=np.float32)
    spread = np.zeros((H, SPREAD + P), np.float32)
    spread[:, SPREAD:SPREAD + H] = np.eye(H, dtype=np.float32)

    arrays = {
        "x_rows": a["x"].reshape(RG, RGP, D).transpose(1, 0, 2),
        "ctx_nat": ctx_in.reshape(B, PIECES, PCT, CT, D).transpose(0, 1, 3, 2, 4),
        "ctx_tr": ctx_in.reshape(B, PIECES, PT_COLS, DC, P).transpose(0, 1, 4, 3, 2),
        "weights": np.concatenate(tiles),
        "cols": cols,
        "out_bias": np.stack([a["bo1"], a["bo2"], a["b_fc2"]]),
        "key_rows": np.stack([bias_k, bk], axis=1).reshape(LAYERS, 2, H * K),
        "head_rows": np.stack([bias_k, bk, bq]).transpose(2, 0, 1, 3),
        "value_rows": np.stack([bias_v, bv]).transpose(2, 0, 1, 3),
        "ident_in": np.eye(P, dtype=np.float32),
        "mask_in": mask,
        "pick_in": pick,
        "spread_in": spread,
    }
    arrays = {k: np.ascontiguousarray(v) for k, v in arrays.items()}
    nc = bacc.Bacc("TRN2", target_bir_lowering=False, num_devices=1)
    aps = {k: nc.dram_tensor(k, v.shape, F32, kind="ExternalInput").ap() for k, v in arrays.items()}
    out = nc.dram_tensor("out_rows", (RGP, RG, D), F32, kind="ExternalOutput").ap()
    build(nc, **aps, out=out)
    got = run(nc, [arrays], core_ids=[0]).results[0]["out_rows"]
    return got.transpose(1, 0, 2).reshape(B, Q, D)
```

```python
import concourse.bass as bass
from concourse import mybir
from contextlib import ExitStack

F32 = mybir.dt.float32
F32R = mybir.dt.float32r
ALU = mybir.AluOpType
ACT = mybir.ActivationFunctionType
X = mybir.AxisListType.X
ds = bass.ds

LAYERS, B, Q, D, H, K, T, F = 2, 8, 56, 256, 16, 128, 1500, 1024
P = 128
DC = D // P
ROWS = B * Q
RG = 4
RGP = ROWS // RG
FLAT = Q * H
TILES = FLAT // P
TQ = P // H
NT = B * TILES
CT = 125
NCT = T // CT
GRP = 4
NG = NCT // GRP
PIECES = 4
PCT = NCT // PIECES
PT_COLS = T // PIECES
BANK = 512
SPANS = [(0, BANK), (BANK, 2 * BANK), (2 * BANK, T)]
FT = F // P
QUADS = H // 4
JOBS = 2 * H
SCALE = float(K) ** -0.5
LN_EPS = 1e-5
HI, LO = 0, 1
TERMS = ((HI, HI), (HI, LO), (LO, HI))

COL_LN = 0
COL_BQ = COL_LN + 3 * 2 * DC
COL_BV = COL_BQ + LAYERS * H
COL_B1 = COL_BV + LAYERS * H
N_COLS = COL_B1 + FT
INIT = 4
LN_CHAIN = 4
EXTRA = 80
SPREAD = (TQ - 1) * H


def build(nc, x_rows, ctx_nat, ctx_tr, weights, cols, out_bias, head_rows, value_rows,
          ident_in, mask_in, pick_in, spread_in, dk_rows, out):
    stack = ExitStack()
    with stack:
        place_at = [(nc.sbuf_base + 63) // 64 * 64]

        def sb(name, shape, dtype):
            size = 4
            for n in shape[1:]:
                size *= n
            at = place_at[0]
            place_at[0] += (size + 31) // 32 * 32
            return nc.alloc_sbuf_tensor_at(name, shape, dtype, offset=at)

        def sem(name):
            return stack.enter_context(nc.semaphore(name))

        qt_at = place_at[0]
        qt = sb("qt", [P, DC, B, FLAT], F32)
        nat_stage = sb("nat_stage", [CT, PCT, D], F32)
        tr_stage = sb("tr_stage", [P, DC, PT_COLS], F32)
        xres = sb("xres", [RGP, RG, D], F32)
        w_raw = [sb(f"w_raw{u}", [P, 2 * D], F32) for u in range(2)]
        w = [sb(f"w{u}", [P, 2, 2 * D], F32R) for u in range(2)]
        ident = sb("ident", [P, P], F32)
        col = sb("col", [P, N_COLS], F32)
        bo = sb("bo", [RGP, 3, D], F32)
        lb = sb("lb", [P, NT], F32)
        neg_max = sb("neg_max", [P, NT], F32)
        row_sum = sb("row_sum", [P, NT], F32)
        p_extra = sb("p_extra", [P, NT], F32)
        den = sb("den", [P, NT], F32)
        rden = sb("rden", [P, NT], F32)
        pn_extra = sb("pn_extra", [P, NT], F32)
        mx = sb("mx", [P, 4], F32)
        part_sum = sb("part_sum", [P, NG], F32)
        g_cols = sb("g_cols", [P, DC, H], F32)
        cq = sb("cq", [H, LAYERS], F32)
        dv = sb("dv", [EXTRA, LAYERS, K], F32)
        mask = sb("mask", [EXTRA, H], F32)
        pick = sb("pick", [P, TQ, EXTRA], F32)
        spread = sb("spread", [H, SPREAD + P], F32)
        ln_stat = sb("ln_stat", [RGP, RG, 6], F32)
        ln_mv = sb("ln_mv", [RGP, RG, 2], F32)
        ln_v = sb("ln_v", [RGP, RG], F32)
        minus_half = sb("minus_half", [RGP, RG], F32)
        ln_y = sb("ln_y", [RGP, RG], F32)
        ln_t = sb("ln_t", [RGP, RG], F32)
        ln_u = sb("ln_u", [RGP, RG], F32)
        ln_r = sb("ln_r", [RGP, RG], F32)
        p80 = sb("p80", [EXTRA, ROWS], F32R)

        at_pt = place_at[0]
        pt = sb("pt", [CT, 2, NG, GRP * P], F32R)
        at_attention = place_at[0]
        place_at[0] = at_pt
        w_raw += [sb(f"w_raw{u}", [P, 2 * D], F32) for u in (2, 3)]
        dk_all = sb("dk_all", [P, H * K], F32)
        assert place_at[0] <= at_attention
        place_at[0] = at_attention
        e = sb("e", [P, T + 4], F32)
        on = sb("on", [P, D], F32)
        on_lo = sb("on_lo", [P, D], F32)
        qs = sb("qs", [P, 2, DC, P], F32R)
        after_attention = place_at[0]
        place_at[0] = at_attention
        g_prod = [sb(f"g_prod{s}", [P, DC, K], F32) for s in range(2)]
        w += [sb(f"w{u}", [P, 2, 2 * D], F32R) for u in (2, 3)]
        place_at[0] = max(place_at[0], after_attention)

        N_TR, N_NAT = DC * 2 * T, NCT * 2 * D
        slot_words = N_TR + N_NAT
        ctx = sb("ctx", [P, 2, slot_words], F32R)
        end = place_at[0]
        assert end <= nc.sbuf_usable_end, (end, nc.sbuf_usable_end)

        scratch_at = end - slot_words * 4
        place_at[0] = scratch_at
        xn = sb("xn", [RGP, RG, D], F32)
        ht32 = sb("ht32", [P, DC, ROWS], F32)
        ht = sb("ht", [P, 2, DC, ROWS], F32R)
        after_ln = place_at[0]
        qh = [sb(f"qh{u}", [P, 2, ROWS], F32R) for u in range(4)]
        lb_rows = sb("lb_rows", [H, ROWS], F32)
        assert place_at[0] <= end, (place_at[0], end)
        place_at[0] = after_ln
        cs = [sb(f"cs{u}", [P, 2, ROWS], F32R) for u in range(4)]
        pm = [sb(f"pm{s}", [EXTRA, ROWS], F32R) for s in range(2)]
        dv80 = sb("dv80", [EXTRA, K], F32R)
        oth_at = place_at[0]
        oth = [sb(f"oth{s}", [P, 2, DC, ROWS], F32R) for s in range(2)]
        assert place_at[0] <= end
        place_at[0] = oth_at
        g32 = [sb(f"g32_{s}", [P, ROWS], F32) for s in range(2)]
        assert place_at[0] <= end
        place_at[0] = qt_at
        hrow = sb("hrow", [H, 3, LAYERS, K], F32)
        vrow = sb("vrow", [EXTRA, 2, LAYERS, K], F32)
        hdiff = sb("hdiff", [H, LAYERS, K], F32)
        hprod = sb("hprod", [H, LAYERS, K], F32)

        logits = stack.enter_context(nc.psum_tensor("logits", [P, 3 * BANK], F32))
        single = [stack.enter_context(nc.psum_tensor(f"bank{i}", [P, BANK], F32)) for i in range(3, 8)]
        bank = [logits[:, i * BANK:(i + 1) * BANK] for i in range(3)] + [t[:, :] for t in single]
        TP = [bank[3], bank[4], bank[7]]
        O_BANK, OT_BANK = bank[5], bank[6]
        LN_BANK = [bank[6], bank[7]]
        Q_BANK = [bank[3], bank[4], bank[2], bank[7]]
        QP_BANK = [[bank[5], bank[6]], [bank[0], bank[1]]]
        C_BANK = [bank[3], bank[4], bank[6], bank[7]]
        Y_BANK = [bank[0], bank[1], bank[2], bank[5]]

        zeroed = sem("zeroed")
        x_in = [sem(f"x_in{g}") for g in range(RG)]
        tables_in, consts_in = sem("tables_in"), sem("consts_in")
        setup_step = sem("setup_step")
        cq_step, cq_ready, dv_ready = sem("cq_step"), sem("cq_ready"), sem("dv_ready")
        nat_in, tr_in = sem("nat_in"), sem("tr_in")
        nat_hi, nat_lo, tr_hi, tr_lo = sem("nat_hi"), sem("nat_lo"), sem("tr_hi"), sem("tr_lo")
        w_in = [sem(f"w_in{u}") for u in range(4)]
        w_hi, w_lo, w_used = sem("w_hi"), sem("w_lo"), sem("w_used")
        hrow_in, vrow_in = sem("hrow_in"), sem("vrow_in")
        dk_ready, dk_written = sem("dk_ready"), sem("dk_written")
        dk_first_in, dk_rest_in = sem("dk_first_in"), sem("dk_rest_in")
        gp_ready, gp_used = sem("gp_ready"), sem("gp_used")
        ln_stats, ln_aggr, ln_chain, ln_pow = sem("ln_stats"), sem("ln_aggr"), sem("ln_chain"), sem("ln_pow")
        xn_ready, xt_mm = sem("xn_ready"), sem("xt_mm")
        h32_ready, h_hi, h_lo = sem("h32_ready"), sem("h_hi"), sem("h_lo")
        q_mm, q_hi, q_lo = sem("q_mm"), sem("q_hi"), sem("q_lo")
        qp_mm, qp_out = sem("qp_mm"), sem("qp_out")
        lb_mm, lb_rows_ready, lb_spread, lb_ready = (
            sem("lb_mm"), sem("lb_rows_ready"), sem("lb_spread"), sem("lb_ready"))
        qs_hi, qs_lo = sem("qs_hi"), sem("qs_lo")
        first_qs_hi, first_qs_lo = sem("first_qs_hi"), sem("first_qs_lo")
        s_mm = sem("s_mm")
        mx_step, max_ready = sem("mx_step"), sem("max_ready")
        exp_part, exp_done, pe_done = sem("exp_part"), sem("exp_done"), sem("pe_done")
        sum_ready = sem("sum_ready")
        den_ready, rden_ready, pn_ready = sem("den_ready"), sem("rden_ready"), sem("pn_ready")
        tp_mm, pt_hi, pt_lo = sem("tp_mm"), sem("pt_hi"), sem("pt_lo")
        pv_mm, onlo_ready, on_ready = sem("pv_mm"), sem("onlo_ready"), sem("on_ready")
        ot_mm, ot_out = sem("ot_mm"), sem("ot_out")
        pn_picked = sem("pn_picked")
        dv80_step, p80_hi, p80_lo = sem("dv80_step"), sem("p80_hi"), sem("p80_lo")
        pm_ready, oth_hi, oth_lo = sem("pm_ready"), sem("oth_hi"), sem("oth_lo")
        c_mm, c_hi, c_lo, g32_ready = sem("c_mm"), sem("c_hi"), sem("c_lo"), sem("g32_ready")
        y_mm, xb_ready, x_ready = sem("y_mm"), sem("xb_ready"), sem("x_ready")
        out_written = sem("out_written")
        settled = sem("settled")

        N_TABLES, N_CONSTS = 2, 4

        def settle(eng):
            eng.sem_inc(settled, 1)

        started_by = {
            "pe": [w_used, xt_mm, q_mm, qp_mm, lb_mm, lb_spread, s_mm, tp_mm, pv_mm, ot_mm, pn_picked, c_mm, y_mm],
            "act": [w_hi, h_hi, q_hi, qp_out, first_qs_hi, exp_part, exp_done, pe_done, pt_hi, onlo_ready, ot_out,
                    p80_hi, oth_hi, c_hi, g32_ready],
            "dve": [x_ready, ln_stats, ln_aggr, ln_chain, xn_ready, h32_ready, h_lo, dk_ready, cq_step, cq_ready,
                    dv_ready, gp_ready, gp_used, q_lo, first_qs_lo, lb_rows_ready, nat_hi, tr_hi, lb_ready, mx_step,
                    max_ready, sum_ready, den_ready, rden_ready, pn_ready, pt_lo, on_ready, p80_lo, oth_lo, c_lo,
                    xb_ready],
            "pool": [zeroed, setup_step, nat_lo, tr_lo, w_lo, ln_pow, qs_hi, qs_lo, dv80_step, pm_ready],
        }

        def start(eng, name):
            for counter in started_by[name]:
                eng.sem_inc(counter, INIT)

        qt_flat = qt[:].rearrange("p c b f -> p c (b f)")

        def head_rows_of(h):
            return qt[:].rearrange("p c b (q h) -> p c (b q) h", h=H)[:, :, :, ds(h, 1)].rearrange(
                "p c r a -> p c (r a)")

        def ctx_tr_part(slot, half, part, lo, hi):
            at = (half * 2 + part) * T
            return ctx[:, ds(slot, 1), at + lo:at + hi].rearrange("p a t -> p (a t)")

        def ctx_nat_tile(slot, t, width):
            at = N_TR + t * 2 * D
            return ctx[0:CT, ds(slot, 1), at:at + width].rearrange("p a t -> p (a t)")

        def as_f32(ap):
            return ap.bitcast(F32)

        def piece_views(slot, p):
            nat = ctx[0:CT, ds(slot, 1), ds(p * (PCT * 2 * D) + N_TR, PCT * 2 * D)].rearrange(
                "p a (t c d) -> p (a t) c d", t=PCT, c=2)
            tr = ctx[:, ds(slot, 1), 0:N_TR].rearrange("p a (c h t) -> p (a c) h t", c=DC, h=2)
            return nat, tr[:, :, :, ds(p * PT_COLS, PT_COLS)]

        block = stack.enter_context(nc.Block())

        @block.sync
        def _(sp):
            def load_weight(job, u, products):
                sp.wait_ge(w_lo, INIT + job - 3)
                settle(sp)
                if products is not None:
                    sp.wait_ge(gp_ready, INIT + products)
                    settle(sp)
                sp.dma_start(w_raw[u][:], weights[ds(job, 1)].rearrange("a p n -> (a p) n")).then_inc(w_in[u], 16)

            def load_nat(batch, n, p):
                sp.wait_ge(nat_lo, INIT + n)
                settle(sp)
                sp.dma_start(nat_stage[:], ctx_nat[ds(batch, 1), ds(p, 1)].rearrange(
                    "a b t c d -> (a b t) c d")).then_inc(nat_in, 16)

            def load_tr(batch, n, p):
                sp.wait_ge(tr_lo, INIT + n)
                settle(sp)
                sp.dma_start(tr_stage[:], ctx_tr[ds(batch, 1), ds(p, 1)].rearrange(
                    "a b p c t -> (a b p) c t")).then_inc(tr_in, 16)

            sp.dma_start(hrow[:], head_rows).then_inc(hrow_in, 16)
            for g in range(RG):
                sp.dma_start(xres[:, g], x_rows[:, g]).then_inc(x_in[g], 16)
            sp.dma_start(ident[:], ident_in).then_inc(tables_in, 16)
            sp.dma_start(col[:], cols).then_inc(tables_in, 16)
            for u in range(2):
                sp.dma_start(w_raw[u][:], weights[u]).then_inc(w_in[u], 16)
            sp.wait_ge(dk_ready, INIT + 1)
            sp.dma_start(dk_rows.rearrange("l (h k) -> h l k", h=H), hdiff[:]).then_inc(dk_written, 16)
            sp.wait_ge(zeroed, INIT + 1)
            for g in range(3):
                sp.dma_start(vrow[32 * g:32 * g + H], value_rows).then_inc(vrow_in, 16)
            for u in range(2, 4):
                sp.dma_start(w_raw[u][:], weights[u]).then_inc(w_in[u], 16)
            sp.dma_start(bo[:], out_bias.partition_broadcast(RGP)).then_inc(consts_in, 16)
            sp.dma_start(mask[:], mask_in).then_inc(consts_in, 16)
            sp.dma_start(pick[:], pick_in).then_inc(consts_in, 16)
            sp.dma_start(spread[:], spread_in).then_inc(consts_in, 16)
            sp.wait_ge(dk_written, 16)
            with sp.Fori(0, LAYERS) as l:
                sp.wait_ge(pv_mm, INIT + l * NT)
                settle(sp)
                for heads, arrived in ((slice(0, 4 * K), dk_first_in), (slice(4 * K, H * K), dk_rest_in)):
                    sp.dma_start(dk_all[:, heads], dk_rows[ds(l, 1), heads].rearrange(
                        "a n -> (a n)").partition_broadcast(P)).then_inc(arrived, 16)
                with sp.Fori(0, QUADS - 1) as quad:
                    for u in range(4):
                        load_weight(l * JOBS + quad * 4 + (u + 4), u, l * H + quad * 4 + (u + 1))
                        if u == 0:
                            load_nat(0, l * (B * PIECES) + quad, quad)
                        if u == 2:
                            load_tr(0, l * (B * PIECES) + quad, quad)
                for u in range(2):
                    load_weight(l * JOBS + (H + u), u, l * H + (H - 3 + u))
                load_nat(0, l * (B * PIECES) + PIECES - 1, PIECES - 1)
                load_tr(0, l * (B * PIECES) + PIECES - 1, PIECES - 1)

                with sp.Fori(0, B - 1) as b:
                    for p in range(PIECES):
                        load_nat(b + 1, l * (B * PIECES) + b * PIECES + PIECES + p, p)
                        load_tr(b + 1, l * (B * PIECES) + b * PIECES + PIECES + p, p)

                sp.wait_ge(pv_mm, INIT + (l + 1) * NT)
                settle(sp)
                for u in range(2, 4):
                    load_weight(l * JOBS + (H + u), u, l * H + (H - 3 + u))
                with sp.Fori(0, QUADS) as quad:
                    for u in range(4):
                        load_weight(l * JOBS + quad * 4 + (H + 4 + u), u, None)

            for u in range(4):
                load_weight(LAYERS * JOBS + 4 + u, u, None)

            for g in range(RG):
                sp.wait_ge(x_ready, INIT + 2 * RG + g + 1)
                sp.dma_start(out[:, g], xres[:, g]).then_inc(out_written, 16)
            sp.wait_ge(out_written, RG * 16)

        @block.gpsimd
        def _(pool):
            def weight_lo(job, u):
                pool.wait_ge(w_hi, INIT + job + 1)
                settle(pool)
                nc.gpsimd.tensor_tensor(w[u][:, LO, :], w_raw[u][:], as_f32(w[u][:, HI, :]),
                                        ALU.subtract).then_inc(w_lo, 1)

            def nat_part_lo(slot, n, p):
                nat, _ = piece_views(slot, p)
                pool.wait_ge(nat_hi, INIT + n + 1)
                settle(pool)
                nc.gpsimd.tensor_tensor(nat[:, :, LO, :], nat_stage[:], as_f32(nat[:, :, HI, :]),
                                        ALU.subtract).then_inc(nat_lo, 1)

            def tr_part_lo(slot, n, p):
                _, tr = piece_views(slot, p)
                pool.wait_ge(tr_hi, INIT + n + 1)
                settle(pool)
                nc.gpsimd.tensor_tensor(tr[:, :, LO, :], tr_stage[:], as_f32(tr[:, :, HI, :]),
                                        ALU.subtract).then_inc(tr_lo, 1)

            def split_q(tile, n):
                src = qt_flat[:, :, ds(tile * P, P)]
                nc.gpsimd.tensor_copy(qs[:, HI], src).then_inc(qs_hi, 1)
                pool.wait_ge(qs_hi, INIT + n + 1)
                settle(pool)
                nc.gpsimd.tensor_tensor(qs[:, LO], src, as_f32(qs[:, HI]), ALU.subtract).then_inc(qs_lo, 1)

            def norm(m):
                pool.wait_ge(ln_chain, INIT + m * LN_CHAIN + 1)
                settle(pool)
                nc.gpsimd.tensor_tensor(ln_y[:], ln_v[:], minus_half[:], ALU.pow).then_inc(ln_pow, 1)

            start(pool, "pool")
            nc.gpsimd.memset(vrow[:], 0.0).then_inc(zeroed, 1)
            nc.gpsimd.memset(minus_half[:], -0.5).then_inc(setup_step, 1)
            pool.wait_ge(setup_step, INIT + 1)
            settle(pool)

            norm(0)
            for u in range(4):
                weight_lo(u, u)

            with pool.Fori(0, LAYERS) as l:
                with pool.Fori(0, QUADS - 1) as quad:
                    for u in range(4):
                        weight_lo(l * JOBS + quad * 4 + (u + 4), u)
                        if u == 1:
                            nat_part_lo(0, l * (B * PIECES) + quad, quad)
                    tr_part_lo(0, l * (B * PIECES) + quad, quad)
                for u in range(2):
                    weight_lo(l * JOBS + (H + u), u)
                nat_part_lo(0, l * (B * PIECES) + PIECES - 1, PIECES - 1)
                tr_part_lo(0, l * (B * PIECES) + PIECES - 1, PIECES - 1)

                pool.wait_ge(s_mm, INIT + (l * NT + 1) * 3)
                settle(pool)
                split_q(1, l * (NT - 1))

                def next_q(b, r):
                    n = l * NT + b * TILES + (r + 2)
                    pool.wait_ge(s_mm, INIT + n * 3)
                    settle(pool)
                    split_q(b * TILES + (r + 2), l * (NT - 1) + b * TILES + (r + 1))

                next_q(0, 0)
                with pool.Fori(0, B - 1) as b:
                    for r in range(1, TILES + 1):
                        next_q(b, r)
                        if r <= PIECES:
                            piece = ((b + 1) & 1, l * (B * PIECES) + b * PIECES + PIECES + r - 1, r - 1)
                            nat_part_lo(*piece)
                            tr_part_lo(*piece)
                for r in range(1, TILES - 2):
                    next_q(B - 1, r)

                pool.wait_ge(pv_mm, INIT + (l + 1) * NT)
                settle(pool)
                pool.wait_ge(dv_ready, INIT + 1)
                dv_l = dv[:, ds(l, 1), :].rearrange("p a k -> p (a k)")
                nc.gpsimd.tensor_copy(dv80[:], dv_l).then_inc(dv80_step, 1)
                pool.wait_ge(dv80_step, INIT + l * 2 + 1)
                settle(pool)
                nc.gpsimd.tensor_tensor(dv80[32:64], dv_l[32:64], as_f32(dv80[32:64]),
                                        ALU.subtract).then_inc(dv80_step, 1)
                pool.wait_ge(dv80_step, INIT + l * 2 + 2)

                def mask_extra(h, s, free):
                    pool.wait_ge(c_mm, INIT + free)
                    settle(pool)
                    nc.gpsimd.tensor_tensor(pm[s][:], as_f32(p80[:]), mask[:, ds(h, 1)].to_broadcast([EXTRA, ROWS]),
                                            ALU.mult).then_inc(pm_ready, 1)

                pool.wait_ge(consts_in, 16 * N_CONSTS)
                pool.wait_ge(p80_lo, INIT + l + 1)
                for s in range(2):
                    mask_extra(s, s, l * H)
                for u in range(2, 4):
                    weight_lo(l * JOBS + (H + u), u)
                    mask_extra(u, u - 2, l * H + (u - 1))
                with pool.Fori(0, QUADS - 1) as quad:
                    for u in range(4):
                        weight_lo(l * JOBS + quad * 4 + (H + 4 + u), u)
                        mask_extra(quad * 4 + (u + 4), u % 2, l * H + quad * 4 + (u + 3))
                for u in range(2):
                    weight_lo((l + 1) * JOBS + u, u)
                norm(l + 1)
                for u in range(2, 4):
                    weight_lo((l + 1) * JOBS + u, u)

            for u in range(4):
                weight_lo(LAYERS * JOBS + 4 + u, u)

        @block.tensor
        def _(pe):
            mm = nc.tensor.matmul

            def norm_transposes(m):
                for g in range(RG):
                    pe.wait_ge(xn_ready, INIT + m * RG + g + 1)
                    settle(pe)
                    for c in range(DC):
                        last = nc.tensor.transpose(LN_BANK[c][:, g * RGP:(g + 1) * RGP],
                                                   xn[:, g, c * P:(c + 1) * P], ident[0:RGP, 0:RGP])
                        if g == RG - 1:
                            last.then_inc(xt_mm, 1)

            def project(out_bank, u, moving, ready, more):
                for m, terms in ((HI, (HI, LO)), (LO, (HI,))):
                    counter, value, step = ready[m]
                    for c in range(DC):
                        if c == 0 or step:
                            pe.wait_ge(counter, value + c * step)
                        for a in terms:
                            last = mm(out_bank, w[u][:, a, c * P:(c + 1) * P], moving(m, c),
                                      start=(m, c, a) == (HI, 0, HI), stop=(not more and (m, c) == (LO, DC - 1)))
                return last

            def h_ready(m):
                return (h_hi, INIT + m * DC + 1, 1), (h_lo, INIT + m * DC + 1, 1)

            def queries(u, n, job):
                pe.wait_ge(w_lo, INIT + job + 1)
                pe.wait_ge(q_lo, INIT + n - 3)
                project(Q_BANK[u][:, 0:ROWS], u, lambda m, c: ht[:, m, c, :], h_ready(l), False).then_inc(q_mm, 1)

            def carried_queries(u, n):
                bank_of = QP_BANK[u % 2]
                pe.wait_ge(qp_out, INIT + 2 * (n - 1))
                pe.wait_ge(q_lo, INIT + n + 1)
                for c in range(DC):
                    for a, m in TERMS:
                        last = mm(bank_of[c][:, 0:ROWS], w[u][:, a, D + c * P:D + (c + 1) * P], qh[u][:, m, :],
                                  start=(a, m) == (HI, HI), stop=(a, m) == (LO, HI))
                    last.then_inc(qp_mm if c == 0 else w_used, 1)

            def exp_transposes(g, n):
                for j in range(GRP):
                    t = g * GRP + j
                    last = nc.tensor.transpose(TP[g][0:CT, j * P:(j + 1) * P], e[:, t * CT:(t + 1) * CT], ident[:])
                last.then_inc(tp_mm, 1)

            def logit_bank(k, slot):
                lo, hi = SPANS[k]
                terms = [(c, a, m) for c in range(DC) for a, m in TERMS]
                for c, a, m in terms:
                    last = mm(logits[:, lo:hi], qs[:, a, c, :], ctx_tr_part(slot, c, m, lo, hi),
                              start=(c, a, m) == terms[0], stop=(c, a, m) == terms[-1])
                last.then_inc(s_mm, 1)

            def weighted_context(slot, n):
                pe.wait_ge(on_ready, INIT + n)
                for g in range(NG):
                    pe.wait_ge(pt_lo, INIT + n * NG + g + 1)
                    for j in range(GRP):
                        t = g * GRP + j
                        mm(O_BANK[:, 0:2 * D], pt[:, HI, g, j * P:(j + 1) * P], ctx_nat_tile(slot, t, 2 * D),
                           start=(t == 0), stop=(t == NCT - 1), skip_group_check=True)
                        last = mm(O_BANK[:, 0:D], pt[:, LO, g, j * P:(j + 1) * P], ctx_nat_tile(slot, t, D),
                                  start=False, stop=(t == NCT - 1), skip_group_check=True)
                last.then_inc(pv_mm, 1)

            def context_transposes(n):
                pe.wait_ge(on_ready, INIT + n + 1)
                pe.wait_ge(ot_out, INIT + n)
                for c in range(DC):
                    last = nc.tensor.transpose(OT_BANK[:, c * P:(c + 1) * P], on[:, c * P:(c + 1) * P], ident[:])
                last.then_inc(ot_mm, 1)

            def head_context(u, n, job, extra):
                s = u % 2
                pe.wait_ge(w_lo, INIT + job + 1)
                pe.wait_ge(c_lo, INIT + n - 3)
                if extra:
                    project(C_BANK[u][:, 0:ROWS], u, lambda m, c: oth[s][:, m, c, :],
                            ((oth_hi, INIT + n + 1, 0), (oth_lo, INIT + n + 1, 0)), True)
                    pe.wait_ge(pm_ready, INIT + n + 1)
                    mm(C_BANK[u][:, 0:ROWS], dv80[:], pm[s][:], start=False, stop=True).then_inc(c_mm, 1)
                else:
                    project(C_BANK[u][:, 0:ROWS], u, lambda m, c: ht[:, m, c, :], h_ready(LAYERS),
                            False).then_inc(c_mm, 1)

            def row_group(u, g, first, last_head):
                rows = slice(g * RGP, (g + 1) * RGP)
                for a, m in TERMS:
                    last = mm(Y_BANK[g][0:RGP, 0:D], cs[u][:, a, rows], w[u][:, m, D:2 * D],
                              start=first and (a, m) == (HI, HI), stop=last_head and (a, m) == (LO, HI))
                return last

            def output_rows(u, n, first):
                pe.wait_ge(c_lo, INIT + n + 1)
                for g in range(RG):
                    last = row_group(u, g, first, False)
                last.then_inc(w_used, 1)

            def last_output_rows(n):
                pe.wait_ge(c_lo, INIT + n + 1)
                for g in range(2):
                    row_group(2, g, False, False)
                pe.wait_ge(c_lo, INIT + n + 2)
                for g in range(2):
                    row_group(3, g, False, True).then_inc(y_mm, 1)
                for g in range(2, RG):
                    row_group(2, g, False, False)
                    last = row_group(3, g, False, True)
                    if g == 2:
                        last.then_inc(y_mm, 1)
                last.then_inc(w_used, 2)

            def output_quad(n, job, extra, first, last_quad):
                for u in range(4):
                    if not (last_quad and u >= 2):
                        head_context((u + 2) % 4, n + (u + 2), job + (u + 2), extra)
                        output_rows(u, n + u, first and u == 0)
                if last_quad:
                    last_output_rows(n + 2)

            start(pe, "pe")
            pe.wait_ge(tables_in, 16 * N_TABLES)
            norm_transposes(0)
            with pe.Fori(0, LAYERS) as l:
                def extra_logits():
                    pe.wait_ge(gp_used, INIT + (l + 1) * H)
                    settle(pe)
                    pe.wait_ge(q_lo, INIT + (l + 1) * H)
                    for c in range(DC):
                        last = mm(bank[7][0:H, 0:ROWS], g_cols[:, c, :], ht32[:, c, :],
                                  start=(c == 0), stop=(c == DC - 1))
                    last.then_inc(lb_mm, 1)

                def query_quad(quad, last_quad):
                    for u in range(4):
                        if not (last_quad and u == 3):
                            queries((u + 1) % 4, l * H + quad * 4 + (u + 1), l * JOBS + quad * 4 + (u + 1))
                        if last_quad and u == 3:
                            extra_logits()
                        carried_queries(u, l * H + quad * 4 + u)

                queries(0, l * H, l * JOBS)
                query_quad(0, False)
                with pe.Fori(1, QUADS - 1) as quad:
                    query_quad(quad, False)
                query_quad(QUADS - 1, True)

                tiles = l * NT
                pe.wait_ge(consts_in, 16 * N_CONSTS)
                pe.wait_ge(lb_rows_ready, INIT + l + 1)
                pe.wait_ge(qp_out, INIT + l * (2 * H) + 2 * (H - 1))
                settle(pe)
                by_query = lb_rows[:].rearrange("h (t e) -> h t e", e=TQ)
                for j in range(TQ):
                    at = SPREAD - j * H
                    last = mm(bank[6][:, 0:NT], spread[:, at:at + P], by_query[:, :, j],
                              start=(j == 0), stop=(j == TQ - 1))
                last.then_inc(lb_spread, 1)
                pe.wait_ge(first_qs_lo, INIT + l + 1)
                pe.wait_ge(tr_lo, INIT + l * (B * PIECES) + PIECES)
                for k in range(NG):
                    logit_bank(k, 0)

                def row_tile(tile, slot, next_slot, new_batch, has_next, has_before):
                    n = tiles + tile
                    if has_before:
                        pe.wait_ge(exp_done, INIT + n + 1)
                    pe.wait_ge(pt_lo, INIT + n * NG)
                    if has_next:
                        pe.wait_ge(qs_lo, INIT + l * (NT - 1) + tile + 1)
                    if new_batch is not None:
                        pe.wait_ge(tr_lo, INIT + l * (B * PIECES) + new_batch * PIECES + PIECES)
                    for k in range(NG):
                        if not has_before:
                            counter, before = (exp_done, n) if k == NG - 1 else (exp_part, l * (NG - 1) + k)
                            pe.wait_ge(counter, INIT + before + 1)
                        exp_transposes(k, n)
                        if has_next:
                            logit_bank(k, next_slot)
                        if has_before and k == 0:
                            context_transposes(n - 1)
                    weighted_context(slot, n)

                row_tile(0, 0, 0, None, True, False)
                with pe.Fori(0, B - 1) as b:
                    for r in range(1, TILES + 1):
                        row_tile(b * TILES + r, (b + r // TILES) & 1, (b + (r + 1) // TILES) & 1,
                                 b + 1 if r == TILES - 1 else None, True, True)
                for r in range(1, TILES):
                    row_tile((B - 1) * TILES + r, (B - 1) & 1, (B - 1) & 1, None, r < TILES - 1, True)
                pe.wait_ge(pn_ready, INIT + tiles + NT)
                settle(pe)
                for j in range(TQ):
                    last = mm(bank[7][0:EXTRA, j * NT:(j + 1) * NT], pick[:, j, :], pn_extra[:],
                              start=(j == 0), stop=True, skip_group_check=True)
                last.then_inc(pn_picked, 1)
                context_transposes(tiles + NT - 1)

                heads, jobs = l * H, l * JOBS + H
                for u in range(2):
                    head_context(u, heads + u, jobs + u, True)
                output_quad(heads, jobs, True, True, False)
                with pe.Fori(1, QUADS - 1) as quad:
                    output_quad(heads + quad * 4, jobs + quad * 4, True, False, False)
                output_quad(heads + 4 * (QUADS - 1), jobs + 4 * (QUADS - 1), True, False, True)
                norm_transposes(l + 1)

            for u in range(2):
                head_context(u, LAYERS * H + u, LAYERS * JOBS + u, False)
            output_quad(LAYERS * H, LAYERS * JOBS, False, True, False)
            output_quad(LAYERS * H + 4, LAYERS * JOBS + 4, False, False, True)

        @block.scalar
        def _(act):
            go = nc.scalar.activation

            def weight_hi(job, u, n_raw):
                act.wait_ge(w_in[u], n_raw * 16 + 16)
                act.wait_ge(w_used, INIT + job - 3)
                go(w[u][:, HI, :], w_raw[u][:], ACT.Copy).then_inc(w_hi, 1)

            def norm(m):
                at = m * (2 * DC) + COL_LN
                act.wait_ge(xt_mm, INIT + m * DC + DC)
                go(ht[:, HI, 0, :], LN_BANK[0][:, 0:ROWS], ACT.Identity, bias=col[:, ds(at + DC, 1)],
                   scale=col[:, ds(at, 1)]).then_inc(h_hi, 1)
                act.wait_ge(h32_ready, INIT + m * DC + 1)
                go(ht[:, HI, 1, :], ht32[:, 1, :], ACT.Copy).then_inc(h_hi, 1)

            def exponentials(tile, n):
                at = ds(tile, 1)
                act.wait_ge(max_ready, INIT + n + 1)
                go(e[:, 0:T], logits[:, 0:T], ACT.Exp, bias=neg_max[:, at],
                   accum_out=row_sum[:, at]).then_inc(exp_done, 1)
                go(p_extra[:, at], lb[:, at], ACT.Exp, bias=neg_max[:, at]).then_inc(pe_done, 1)

            def transposed_context(tile, n):
                act.wait_ge(ot_mm, INIT + n + 1)
                go(qt_flat[:, :, ds(tile * P, P)], OT_BANK[:, 0:D].rearrange("p (c r) -> p c r", c=DC),
                   ACT.Copy).then_inc(ot_out, 1)

            start(act, "act")
            act.wait_ge(tables_in, 16 * N_TABLES)
            for u in range(4):
                act.wait_ge(w_in[u], 16)
                go(w[u][:, HI, :], w_raw[u][:], ACT.Copy).then_inc(w_hi, 1)
                if u == 1:
                    norm(0)
            with act.Fori(0, LAYERS) as l:
                def query_hi(u, h):
                    act.wait_ge(q_mm, INIT + l * H + h + 1)
                    go(qh[u][:, HI, :], Q_BANK[u][:, 0:ROWS], ACT.Identity,
                       bias=col[:, ds(l * H + h + COL_BQ, 1)]).then_inc(q_hi, 1)

                def query_quad(quad, last_quad):
                    for u in range(4):
                        h = quad * 4 + u
                        if not (last_quad and u == 3):
                            query_hi((u + 1) % 4, quad * 4 + (u + 1))
                        act.wait_ge(qp_mm, INIT + l * H + h + 1)
                        for c in range(DC):
                            if c == 1:
                                act.wait_ge(w_used, INIT + l * JOBS + h + 1)
                            go(head_rows_of(h)[:, c], QP_BANK[u % 2][c][:, 0:ROWS],
                               ACT.Copy, scale=SCALE).then_inc(qp_out, 1)
                        if not (last_quad and u >= 2):
                            weight_hi(l * JOBS + quad * 4 + (u + 4), u, l * 8 + quad + 1)

                query_hi(0, 0)
                with act.Fori(0, QUADS - 1) as quad:
                    query_quad(quad, False)
                query_quad(QUADS - 1, True)
                act.wait_ge(qp_out, INIT + (l + 1) * (2 * H))
                act.wait_ge(gp_used, INIT + (l + 1) * H)
                go(qs[:, HI], qt_flat[:, :, 0:P], ACT.Copy).then_inc(first_qs_hi, 1)

                tiles = l * NT
                act.wait_ge(lb_ready, INIT + l + 1)
                act.wait_ge(max_ready, INIT + tiles + 1)
                for k, (lo, hi) in enumerate(SPANS):
                    go(e[:, lo:hi], logits[:, lo:hi], ACT.Exp, bias=neg_max[:, 0:1],
                       accum_out=part_sum[:, k:k + 1]).then_inc(exp_done if k == NG - 1 else exp_part, 1)
                go(p_extra[:, 0:1], lb[:, 0:1], ACT.Exp, bias=neg_max[:, 0:1]).then_inc(pe_done, 1)

                def row_tile(b, r, has_next, has_before):
                    n = tiles + b * TILES + r
                    for g in range(NG):
                        act.wait_ge(tp_mm, INIT + n * NG + g + 1)
                        go(pt[:, HI, g, :], TP[g][0:CT, :], ACT.Copy).then_inc(pt_hi, 1)
                        if g == 1 and has_before:
                            transposed_context(b * TILES + (r - 1), n - 1)
                    if has_next:
                        exponentials(b * TILES + (r + 1), n + 1)
                    act.wait_ge(pv_mm, INIT + n + 1)
                    act.wait_ge(rden_ready, INIT + n + 1)
                    act.wait_ge(on_ready, INIT + n)
                    go(on_lo[:], O_BANK[:, D:2 * D], ACT.Copy, scale=rden[:, ds(b * TILES + r, 1)]).then_inc(
                        onlo_ready, 1)

                row_tile(0, 0, True, False)
                with act.Fori(0, B - 1) as b:
                    for r in range(1, TILES + 1):
                        row_tile(b, r, True, True)
                for r in range(1, TILES):
                    row_tile(B - 1, r, r < TILES - 1, True)
                act.wait_ge(pn_picked, INIT + l + 1)
                go(p80[:].rearrange("p (t e) -> p t e", e=TQ), bank[7][0:EXTRA, 0:ROWS].rearrange(
                    "p (e t) -> p t e", e=TQ), ACT.Copy).then_inc(p80_hi, 1)
                transposed_context(NT - 1, tiles + NT - 1)
                act.wait_ge(ot_out, INIT + tiles + NT)

                def context_hi(h, s, free):
                    act.wait_ge(c_mm, INIT + free)
                    go(oth[s][:, HI], head_rows_of(h), ACT.Copy).then_inc(oth_hi, 1)

                def head_context(u, h):
                    act.wait_ge(c_mm, INIT + l * H + h + 1)
                    go(cs[u][:, HI, :], C_BANK[u][:, 0:ROWS], ACT.Identity,
                       bias=col[:, ds(l * H + h + COL_BV, 1)]).then_inc(c_hi, 1)

                for s in range(2):
                    context_hi(s, s, l * H)
                for u in range(2, 4):
                    weight_hi(l * JOBS + (H + u), u, l * 8 + 4)
                for u in range(2):
                    head_context(u, u)
                    context_hi(u + 2, u, l * H + (u + 1))

                def output_quad(quad, last_quad):
                    for u in range(4):
                        if not (last_quad and u >= 2):
                            head_context((u + 2) % 4, quad * 4 + (u + 2))
                        if not last_quad:
                            context_hi(quad * 4 + (u + 4), u % 2, l * H + quad * 4 + (u + 3))
                        weight_hi(l * JOBS + quad * 4 + (H + 4 + u), u, l * 8 + quad + 5)

                with act.Fori(0, QUADS - 1) as quad:
                    output_quad(quad, False)
                output_quad(QUADS - 1, True)
                norm(l + 1)

            def gelu(f):
                n = LAYERS * H + f
                act.wait_ge(c_mm, INIT + n + 1)
                act.wait_ge(c_lo, INIT + n - 1)
                go(g32[f % 2][:], C_BANK[f % 4][:, 0:ROWS], ACT.Gelu,
                   bias=col[:, COL_B1 + f:COL_B1 + f + 1]).then_inc(g32_ready, 1)
                act.wait_ge(g32_ready, INIT + f + 1)
                go(cs[f % 4][:, HI, :], g32[f % 2][:], ACT.Copy).then_inc(c_hi, 1)

            for f in range(FT):
                gelu(f)
                if 2 <= f < 6:
                    weight_hi(LAYERS * JOBS + (f + 2), f - 2, LAYERS * 8 + 1)

        @block.vector
        def _(dve):
            V = nc.vector

            def statistics(g):
                V.bn_stats(ln_stat[:, g, :], xres[:, g, :]).then_inc(ln_stats, 1)

            def norm(m, first=False):
                base = m * LN_CHAIN
                for g in range(RG):
                    dve.wait_ge(ln_stats, INIT + m * RG + g + 1)
                    settle(dve)
                    V.bn_aggr(ln_mv[:, g, :], ln_stat[:, g, :]).then_inc(ln_aggr, 1)
                dve.wait_ge(ln_aggr, INIT + m * RG + RG)
                V.tensor_scalar(ln_v[:], ln_mv[:, :, 1], LN_EPS, None, ALU.add).then_inc(ln_chain, 1)
                dve.wait_ge(ln_pow, INIT + m + 1)
                V.scalar_tensor_tensor(ln_t[:], ln_v[:], -0.5, ln_y[:], ALU.mult, ALU.mult).then_inc(ln_chain, 1)
                dve.wait_ge(ln_chain, INIT + base + 2)
                V.tensor_tensor(ln_u[:], ln_t[:], ln_y[:], ALU.mult).then_inc(ln_chain, 1)
                dve.wait_ge(ln_chain, INIT + base + 3)
                V.scalar_tensor_tensor(ln_r[:], ln_u[:], 1.5, ln_y[:], ALU.add, ALU.mult).then_inc(ln_chain, 1)
                dve.wait_ge(ln_chain, INIT + base + 4)
                for g in range(RG):
                    V.tensor_scalar(xn[:, g, :], xres[:, g, :], ln_mv[:, g, 0:1], ln_r[:, g:g + 1],
                                    ALU.subtract, ALU.mult).then_inc(xn_ready, 1)
                if first:
                    dve.wait_ge(tables_in, 16 * N_TABLES)
                for c in (1, 0):
                    dve.wait_ge(xt_mm, INIT + m * DC + DC)
                    if c == 0:
                        dve.wait_ge(h_hi, INIT + m * DC + 1)
                    at = m * (2 * DC) + (COL_LN + c)
                    V.tensor_scalar(ht32[:, c, :], LN_BANK[c][:, 0:ROWS], col[:, ds(at, 1)], col[:, ds(at + DC, 1)],
                                    ALU.mult, ALU.add).then_inc(h32_ready, 1)
                dve.wait_ge(h32_ready, INIT + m * DC + DC)
                for c in range(DC):
                    dve.wait_ge(h_hi, INIT + m * DC + c + 1)
                    V.tensor_tensor(ht[:, LO, c, :], ht32[:, c, :], as_f32(ht[:, HI, c, :]),
                                    ALU.subtract).then_inc(h_lo, 1)

            def add_bias(m):
                for g in range(RG):
                    V.tensor_tensor(xres[:, g, :], xres[:, g, :], bo[:, ds(m, 1), :].rearrange(
                        "p a d -> p (a d)"), ALU.add).then_inc(xb_ready, 1)

            def nat_part_hi(slot, n, p):
                nat, _ = piece_views(slot, p)
                dve.wait_ge(nat_in, n * 16 + 16)
                V.tensor_copy(nat[:, :, HI, :], nat_stage[:]).then_inc(nat_hi, 1)

            def tr_part_hi(slot, n, p):
                _, tr = piece_views(slot, p)
                dve.wait_ge(tr_in, n * 16 + 16)
                V.tensor_copy(tr[:, :, HI, :], tr_stage[:]).then_inc(tr_hi, 1)

            def bank_max(k, n):
                dve.wait_ge(s_mm, INIT + n * 3 + k + 1)
                lo, hi = SPANS[k]
                V.tensor_reduce(mx[:, k:k + 1], logits[:, lo:hi], X, ALU.max).then_inc(mx_step, 1)

            def part_max(tile, n):
                dve.wait_ge(mx_step, INIT + n * 4 + 2)
                V.tensor_scalar(mx[:, 3:4], mx[:, 0:1], mx[:, 1:2], lb[:, ds(tile, 1)],
                                ALU.max, ALU.max).then_inc(mx_step, 1)

            def row_max(tile, n):
                dve.wait_ge(mx_step, INIT + n * 4 + 4)
                V.tensor_scalar(neg_max[:, ds(tile, 1)], mx[:, 2:3], mx[:, 3:4], -1.0,
                                ALU.max, ALU.mult).then_inc(max_ready, 1)

            def denominators(tile, n, first=None):
                at = ds(tile, 1)
                if first is not None:
                    dve.wait_ge(sum_ready, INIT + first + 1)
                dve.wait_ge(exp_done, INIT + n + 1)
                dve.wait_ge(pe_done, INIT + n + 1)
                V.tensor_tensor(den[:, at], row_sum[:, at], p_extra[:, at], ALU.add).then_inc(den_ready, 1)
                dve.wait_ge(den_ready, INIT + n + 1)
                V.reciprocal(rden[:, at], den[:, at]).then_inc(rden_ready, 1)
                dve.wait_ge(rden_ready, INIT + n + 1)
                V.tensor_tensor(pn_extra[:, at], p_extra[:, at], rden[:, at], ALU.mult).then_inc(pn_ready, 1)

            def output_sum(m, jobs, more):
                dve.wait_ge(xb_ready, INIT + m * RG + RG)
                for g in range(RG):
                    if g < RG - 1:
                        dve.wait_ge(y_mm, INIT + m * (RG - 1) + g + 1)
                    else:
                        dve.wait_ge(w_used, INIT + jobs)
                    V.tensor_tensor(xres[:, g, :], Y_BANK[g][0:RGP, 0:D], xres[:, g, :], ALU.add).then_inc(x_ready, 1)
                    if more and g > 0:
                        dve.wait_ge(x_ready, INIT + m * RG + g)
                        statistics(g - 1)
                if more:
                    dve.wait_ge(x_ready, INIT + m * RG + RG)
                    statistics(RG - 1)

            start(dve, "dve")
            dve.wait_ge(hrow_in, 16)
            V.tensor_tensor(hdiff[:], hrow[:, 0], hrow[:, 1], ALU.subtract).then_inc(dk_ready, 1)
            for g in range(RG):
                dve.wait_ge(x_in[g], 16)
                statistics(g)
            norm(0, first=True)
            dve.wait_ge(dk_ready, INIT + 1)
            V.tensor_tensor(hprod[:], hdiff[:], hrow[:, 2], ALU.mult).then_inc(cq_step, 1)
            dve.wait_ge(cq_step, INIT + 1)
            V.tensor_reduce(cq[:], hprod[:], X, ALU.add).then_inc(cq_ready, 1)
            dve.wait_ge(vrow_in, 3 * 16)
            V.tensor_tensor(dv[:], vrow[:, 0], vrow[:, 1], ALU.subtract).then_inc(dv_ready, 1)

            with dve.Fori(0, LAYERS) as l:
                def key_bias_product(h, u, n_raw):
                    s = u % 2
                    dve.wait_ge(w_in[u], n_raw * 16 + 16)
                    V.tensor_tensor(g_prod[s][:], w_raw[u][:, 0:DC * K].rearrange("p (c k) -> p c k", c=DC),
                                    dk_all[:, ds(h * K, K)].rearrange("p (a k) -> p a k", a=1).to_broadcast(
                                        [P, DC, K]), ALU.mult).then_inc(gp_ready, 1)
                    dve.wait_ge(gp_ready, INIT + l * H + h + 1)
                    V.tensor_reduce(g_cols[:, :, ds(h, 1)], g_prod[s][:], X, ALU.add).then_inc(gp_used, 1)

                def query_lo(u, h):
                    dve.wait_ge(q_hi, INIT + l * H + h + 1)
                    V.scalar_tensor_tensor(qh[u][:, LO, :], Q_BANK[u][:, 0:ROWS], col[:, ds(l * H + h + COL_BQ, 1)],
                                           as_f32(qh[u][:, HI, :]), ALU.add, ALU.subtract).then_inc(q_lo, 1)

                def query_quad(quad, last_quad):
                    for u in range(4):
                        h = quad * 4 + u
                        if not (last_quad and u == 3):
                            query_lo((u + 1) % 4, quad * 4 + (u + 1))
                        if not (last_quad and u >= 2):
                            key_bias_product(quad * 4 + (u + 2), (u + 2) % 4, l * 8 + quad + (u + 2) // 4)
                        if u == 1:
                            nat_part_hi(0, l * (B * PIECES) + quad, quad)
                        if u == 3:
                            tr_part_hi(0, l * (B * PIECES) + quad, quad)

                dve.wait_ge(dk_first_in, l * 16 + 16)
                settle(dve)
                for u in range(2):
                    key_bias_product(u, u, l * 8)
                query_lo(0, 0)
                dve.wait_ge(dk_rest_in, l * 16 + 16)
                settle(dve)
                with dve.Fori(0, QUADS - 1) as quad:
                    query_quad(quad, False)
                query_quad(QUADS - 1, True)
                dve.wait_ge(lb_mm, INIT + l + 1)
                dve.wait_ge(cq_ready, INIT + 1)
                V.tensor_scalar(lb_rows[:], bank[7][0:H, 0:ROWS], cq[:, ds(l, 1)], SCALE,
                                ALU.add, ALU.mult).then_inc(lb_rows_ready, 1)

                tiles = l * NT
                dve.wait_ge(first_qs_hi, INIT + l + 1)
                V.tensor_tensor(qs[:, LO], qt_flat[:, :, 0:P], as_f32(qs[:, HI]),
                                ALU.subtract).then_inc(first_qs_lo, 1)
                dve.wait_ge(lb_spread, INIT + l + 1)
                V.tensor_copy(lb[:], bank[6][:, 0:NT]).then_inc(lb_ready, 1)
                for k in range(2):
                    bank_max(k, tiles)
                dve.wait_ge(lb_ready, INIT + l + 1)
                part_max(0, tiles)
                bank_max(2, tiles)
                row_max(0, tiles)

                def row_tile(b, r, has_next, piece=None, first=None):
                    n = tiles + b * TILES + r
                    for g in range(NG):
                        dve.wait_ge(pt_hi, INIT + n * NG + g + 1)
                        V.tensor_tensor(pt[:, LO, g, :], TP[g][0:CT, :], as_f32(pt[:, HI, g, :]),
                                        ALU.subtract).then_inc(pt_lo, 1)
                        if has_next:
                            bank_max(g, n + 1)
                            if g == 1:
                                part_max(b * TILES + (r + 1), n + 1)
                    if has_next:
                        row_max(b * TILES + (r + 1), n + 1)
                    denominators(b * TILES + r, n, first)
                    if piece is not None:
                        nat_part_hi(*piece)
                        tr_part_hi(*piece)
                    dve.wait_ge(onlo_ready, INIT + n + 1)
                    dve.wait_ge(ot_mm, INIT + n)
                    V.scalar_tensor_tensor(on[:], O_BANK[:, 0:D], rden[:, ds(b * TILES + r, 1)], on_lo[:],
                                           ALU.mult, ALU.add).then_inc(on_ready, 1)

                dve.wait_ge(exp_done, INIT + tiles + 1)
                V.tensor_reduce(row_sum[:, 0:1], part_sum[:], X, ALU.add).then_inc(sum_ready, 1)
                row_tile(0, 0, True, first=l)
                with dve.Fori(0, B - 1) as b:
                    for r in range(1, TILES + 1):
                        row_tile(b, r, True, ((b + 1) & 1, l * (B * PIECES) + b * PIECES + PIECES + r - 1, r - 1)
                                 if r <= PIECES else None)
                for r in range(1, TILES):
                    row_tile(B - 1, r, r < TILES - 1)

                def context_lo(h, s):
                    dve.wait_ge(oth_hi, INIT + l * H + h + 1)
                    V.tensor_tensor(oth[s][:, LO], head_rows_of(h), as_f32(oth[s][:, HI]),
                                    ALU.subtract).then_inc(oth_lo, 1)

                def head_context(u, h):
                    dve.wait_ge(c_hi, INIT + l * H + h + 1)
                    V.scalar_tensor_tensor(cs[u][:, LO, :], C_BANK[u][:, 0:ROWS], col[:, ds(l * H + h + COL_BV, 1)],
                                           as_f32(cs[u][:, HI, :]), ALU.add, ALU.subtract).then_inc(c_lo, 1)

                dve.wait_ge(p80_hi, INIT + l + 1)
                p80_l = p80[64:EXTRA].rearrange("p (t e) -> p t e", e=TQ)
                V.tensor_tensor(p80_l, bank[7][64:EXTRA, 0:ROWS].rearrange("p (e t) -> p t e", e=TQ),
                                as_f32(p80_l), ALU.subtract).then_inc(p80_lo, 1)
                for s in range(2):
                    context_lo(s, s)
                for u in range(2):
                    head_context(u, u)
                    context_lo(u + 2, u)

                dve.wait_ge(consts_in, 16 * N_CONSTS)
                add_bias(l)

                def output_quad(quad, last_quad):
                    for u in range(4):
                        if not (last_quad and u >= 2):
                            head_context((u + 2) % 4, quad * 4 + (u + 2))
                        if not last_quad:
                            context_lo(quad * 4 + (u + 4), u % 2)

                with dve.Fori(0, QUADS - 1) as quad:
                    output_quad(quad, False)
                output_quad(QUADS - 1, True)
                output_sum(l, (l + 1) * JOBS, True)
                norm(l + 1)

            for f in range(FT):
                dve.wait_ge(c_hi, INIT + LAYERS * H + f + 1)
                V.tensor_tensor(cs[f % 4][:, LO, :], g32[f % 2][:], as_f32(cs[f % 4][:, HI, :]),
                                ALU.subtract).then_inc(c_lo, 1)
                if f == 1:
                    add_bias(LAYERS)
            output_sum(LAYERS, LAYERS * JOBS + FT, False)


def kernel(**inputs):
    import numpy as np
    import concourse.bacc as bacc
    from concourse.bass_utils import run_bass_kernel_spmd as run

    a = {k.removeprefix("L0_xattn_"): np.asarray(v) for k, v in inputs.items()}

    def both(name):
        return np.stack([a[f"{name}1"], a[f"{name}2"]])

    def wide(wm):
        return wm.reshape(DC, P, -1, P).transpose(2, 1, 0, 3).reshape(-1, P, D)

    def pack(first, second):
        return np.concatenate([first, second], axis=2)

    tiles = []
    for n in "12":
        tiles.append(pack(wide(a["wq" + n]), a["wk" + n].reshape(D, H, K).transpose(1, 2, 0)))
        tiles.append(pack(wide(a["wv" + n]), a["wo" + n].reshape(H, K, D)))
    tiles.append(pack(wide(a["w_fc1"]), a["w_fc2"].reshape(FT, P, D)))

    norms = [a[n + part].reshape(DC, P) for n in ("ln1", "ln2", "ln_mlp") for part in ("_scale", "_offset")]
    cols = np.concatenate([*norms, both("bq").reshape(-1, P), both("bv").reshape(-1, P),
                           a["b_fc1"].reshape(FT, P)]).T
    bias_k, bias_v = both("bias_k").reshape(LAYERS, H, K), both("bias_v").reshape(LAYERS, H, K)
    bk, bv, bq = (both(n).reshape(LAYERS, H, K) for n in ("bk", "bv", "bq"))
    ctx_in = a["ctx_2048"]
    mask = np.zeros((EXTRA, H), np.float32)
    for g in range(3):
        mask[32 * g:32 * g + H] = np.eye(H, dtype=np.float32)

    pick = np.zeros((P, TQ, EXTRA), np.float32)
    for j in range(TQ):
        for g in range(3):
            pick[j * H:(j + 1) * H, j, 32 * g:32 * g + H] = np.eye(H, dtype=np.float32)
    spread = np.zeros((H, SPREAD + P), np.float32)
    spread[:, SPREAD:SPREAD + H] = np.eye(H, dtype=np.float32)

    arrays = {
        "x_rows": a["x"].reshape(RG, RGP, D).transpose(1, 0, 2),
        "ctx_nat": ctx_in.reshape(B, PIECES, PCT, CT, D).transpose(0, 1, 3, 2, 4),
        "ctx_tr": ctx_in.reshape(B, PIECES, PT_COLS, DC, P).transpose(0, 1, 4, 3, 2),
        "weights": np.concatenate(tiles),
        "cols": cols,
        "out_bias": np.stack([a["bo1"], a["bo2"], a["b_fc2"]]),
        "head_rows": np.stack([bias_k, bk, bq]).transpose(2, 0, 1, 3),
        "value_rows": np.stack([bias_v, bv]).transpose(2, 0, 1, 3),
        "ident_in": np.eye(P, dtype=np.float32),
        "mask_in": mask,
        "pick_in": pick,
        "spread_in": spread,
    }
    arrays = {k: np.ascontiguousarray(v) for k, v in arrays.items()}
    nc = bacc.Bacc("TRN2", target_bir_lowering=False, num_devices=1)
    aps = {k: nc.dram_tensor(k, v.shape, F32, kind="ExternalInput").ap() for k, v in arrays.items()}
    out = nc.dram_tensor("out_rows", (RGP, RG, D), F32, kind="ExternalOutput").ap()
    dk_rows = nc.dram_tensor("dk_rows", (LAYERS, H * K), F32, kind="Internal").ap()
    build(nc, **aps, dk_rows=dk_rows, out=out)
    got = run(nc, [arrays], core_ids=[0]).results[0]["out_rows"]
    return got.transpose(1, 0, 2).reshape(B, Q, D)
```
